# Optimizing a Trainium2 kernel written in Bass

```python
import numpy as np
import jax
import jax.numpy as jnp

def _softmax(x, axis=-1):
    return jax.nn.softmax(x, axis=axis)

def _gelu(x):
    return jax.nn.gelu(x, approximate=True)

def _silu(x):
    return jax.nn.silu(x)

def _sigmoid(x):
    return jax.nn.sigmoid(x)

def _layernorm(x, axis=-1, eps=1e-05):
    m = jnp.mean(x, axis=axis, keepdims=True)
    v = jnp.var(x, axis=axis, keepdims=True)
    return (x - m) / jnp.sqrt(v + eps)

def _scatter_add(tgt, idx, src, axis=0):
    return tgt.at[idx].add(src)

def _segment_sum(src, seg, n):
    return jax.ops.segment_sum(src, seg, n)
kernel_name = 'mk_adj_ffn_d1_adj_r2_a7df5e'

def setup_inputs(seed: int=0):
    np.random.seed(seed)
    _w = jnp.asarray

    def _rec_inputs():
        import jax
        import jax.numpy as jnp
        _gk = jax.random.key(seed)
        x = -0.000929 + 1 * jax.random.normal(jax.random.fold_in(_gk, 1), (2048, 128), jnp.float32)
        _w = (1.0 + jnp.arange(2048, dtype=jnp.float32)) ** (-0.5)
        _w = _w / _w.mean()
        _pij = jnp.clip(0.00195312 * _w[:, None] * _w[None, :], 0.0, 1.0)
        _a = jax.random.uniform(jax.random.fold_in(_gk, 2), (2048, 2048)) < _pij
        _a = jnp.logical_or(_a, jnp.eye(2048, dtype=bool))
        _af = _a.astype(jnp.float32)
        adj = _af
        return (x, adj)
    x, adj = _rec_inputs()

    def _L0_gnn_setup():
        import jax, jax.numpy as jnp
        import numpy as np
        ALPHA = 0.2
        NEG_INF = -9000000000000000.0
        LN_EPS = 1e-05
        N = 2048
        IN_F = 128
        OUT_F = 128
        HEADS = 4
        HEAD_DIM = OUT_F // HEADS
        EDGE_PROB = 0.02
        key = jax.random.key(seed)
        kx, ka, kw, kav = jax.random.split(key, 4)
        x = jax.random.normal(kx, (N, IN_F), dtype=jnp.float32)
        adj = jax.random.bernoulli(ka, EDGE_PROB, (N, N)).astype(jnp.float32)
        adj = jnp.maximum(adj, jnp.eye(N, dtype=jnp.float32))

        def xavier(k, shape, gain=1.414):
            fan_in, fan_out = (shape[0], shape[1])
            bound = gain * np.sqrt(6.0 / (fan_in + fan_out))
            return jax.random.uniform(k, shape, jnp.float32, -bound, bound)
        W = xavier(kw, (IN_F, OUT_F))
        a = xavier(kav, (2 * HEAD_DIM, 1))
        gamma = jnp.ones((OUT_F,), dtype=jnp.float32)
        beta = jnp.zeros((OUT_F,), dtype=jnp.float32)
        return {'x': x, 'adj': adj, 'W': W, 'a': a, 'gamma': gamma, 'beta': beta}
    _L0_gnn_all = _L0_gnn_setup()
    _L0_gnn_in = {k: v for k, v in _L0_gnn_all.items() if k in ('W', 'a', 'gamma', 'beta')}
    del _L0_gnn_all

    def _L0_ffn_setup():
        import jax, jax.numpy as jnp
        import numpy as np
        D_MODEL = 128
        N_EXPERTS = 16
        HIDDEN = 256
        SCALE = 0.02
        key = jax.random.key(seed)
        ks = jax.random.split(key, 5)
        x = jax.random.normal(ks[0], (4, 4096, D_MODEL), dtype=jnp.float32)
        gate_w = jax.random.normal(ks[1], (D_MODEL, N_EXPERTS), dtype=jnp.float32) * SCALE
        gate_b = jnp.zeros((N_EXPERTS,), dtype=jnp.float32)
        w1 = jax.random.normal(ks[2], (N_EXPERTS, D_MODEL, HIDDEN), dtype=jnp.float32) * SCALE
        w2 = jax.random.normal(ks[3], (N_EXPERTS, D_MODEL, HIDDEN), dtype=jnp.float32) * SCALE
        w3 = jax.random.normal(ks[4], (N_EXPERTS, HIDDEN, D_MODEL), dtype=jnp.float32) * SCALE
        return {'x': x, 'gate_w': gate_w, 'gate_b': gate_b, 'w1': w1, 'w2': w2, 'w3': w3}
    _L0_ffn_all = _L0_ffn_setup()
    _L0_ffn_in = {k: v for k, v in _L0_ffn_all.items() if k in ('gate_w', 'gate_b', 'w1', 'w2', 'w3')}
    del _L0_ffn_all
    return {'x': x, 'adj': adj, 'L0_gnn_W': _L0_gnn_in['W'], 'L0_gnn_a': _L0_gnn_in['a'], 'L0_gnn_gamma': _L0_gnn_in['gamma'], 'L0_gnn_beta': _L0_gnn_in['beta'], 'L0_ffn_gate_w': _L0_ffn_in['gate_w'], 'L0_ffn_gate_b': _L0_ffn_in['gate_b'], 'L0_ffn_w1': _L0_ffn_in['w1'], 'L0_ffn_w2': _L0_ffn_in['w2'], 'L0_ffn_w3': _L0_ffn_in['w3']}

def reference(x, adj, L0_gnn_W, L0_gnn_a, L0_gnn_gamma, L0_gnn_beta, L0_ffn_gate_w, L0_ffn_gate_b, L0_ffn_w1, L0_ffn_w2, L0_ffn_w3):
    import jax
    import jax.numpy as jnp

    def _L0_gnn_ref(x, adj, W, a, gamma, beta):
        import jax, jax.numpy as jnp
        import numpy as np
        ALPHA = 0.2
        NEG_INF = -9000000000000000.0
        LN_EPS = 1e-05
        N = 2048
        IN_F = 128
        OUT_F = 128
        HEADS = 4
        HEAD_DIM = OUT_F // HEADS
        EDGE_PROB = 0.02
        n = x.shape[0]
        head_dim = a.shape[0] // 2
        heads = W.shape[1] // head_dim
        h = (x @ W).reshape(n, heads, head_dim)
        src = jnp.einsum('nhd,d->nh', h, a[:head_dim, 0])
        dst = jnp.einsum('nhd,d->nh', h, a[head_dim:, 0])
        e = src[:, :, None] + dst.T[None, :, :]
        e = jnp.where(e > 0, e, ALPHA * e)
        mask = adj[:, None, :] > 0
        e = jnp.where(mask, e, NEG_INF)
        attn = jax.nn.softmax(e, axis=-1)
        out = jnp.einsum('nhm,mhd->nhd', attn, h)
        out = out.reshape(n, heads * head_dim)
        mu = jnp.mean(out, axis=-1, keepdims=True)
        var = jnp.var(out, axis=-1, keepdims=True)
        out = (out - mu) / jnp.sqrt(var + LN_EPS) * gamma + beta
        return out

    def _L0_ffn_ref(x, gate_w, gate_b, w1, w2, w3):
        import jax, jax.numpy as jnp
        import numpy as np
        D_MODEL = 128
        N_EXPERTS = 16
        HIDDEN = 256
        SCALE = 0.02
        n_experts = w1.shape[0]
        logits = jnp.einsum('bsd,de->bse', x, gate_w) + gate_b
        probs = jax.nn.softmax(logits, axis=-1)
        top_probs, top_idx = jax.lax.top_k(probs, 2)
        top_probs = top_probs / jnp.sum(top_probs, axis=-1, keepdims=True)
        dispatch = jnp.sum(jax.nn.one_hot(top_idx, n_experts, dtype=x.dtype) * top_probs[..., None], axis=-2)
        h1 = jnp.einsum('bsd,edh->bseh', x, w1)
        h2 = jnp.einsum('bsd,edh->bseh', x, w2)
        hidden = jax.nn.silu(h1) * h2
        expert_out = jnp.einsum('bseh,eho->bseo', hidden, w3)
        return jnp.einsum('bseo,bse->bso', expert_out, dispatch)
    x = x + _L0_gnn_ref(_layernorm(x, axis=-1), adj, L0_gnn_W, L0_gnn_a, L0_gnn_gamma, L0_gnn_beta)
    x = x + _L0_ffn_ref(_layernorm(x, axis=-1)[None], L0_ffn_gate_w, L0_ffn_gate_b, L0_ffn_w1, L0_ffn_w2, L0_ffn_w3)[0]
    return x

_drawn_inputs = setup_inputs


def setup_inputs(seed=0):
    import zlib

    import numpy as np

    out = dict(_drawn_inputs(seed))
    spreads = {'L0_gnn_gamma': (1.0, 0.2), 'L0_gnn_beta': (0.0, 0.1), 'L0_ffn_gate_b': (0.0, 0.8)}
    factors = {'L0_ffn_gate_w': 8.0, 'L0_ffn_w1': 8.0, 'L0_ffn_w2': 8.0, 'L0_ffn_w3': 8.0}
    for name, (base, spread) in spreads.items():
        noise = np.random.default_rng([zlib.crc32(name.encode()), seed]).standard_normal(out[name].shape)
        drawn = base * np.exp(spread * noise) if base else spread * noise
        out[name] = jnp.asarray(drawn.astype(out[name].dtype))
    for name, factor in factors.items():
        out[name] = (out[name] * factor).astype(out[name].dtype)
    return out
```

```python
from contextlib import ExitStack

import concourse.bass as bass
from concourse import mybir

F32 = mybir.dt.float32
BF16 = mybir.dt.bfloat16
I32 = mybir.dt.int32
ALU = mybir.AluOpType
ACT = mybir.ActivationFunctionType
AX = mybir.AxisListType

P = 128
EPS = 1e-5
SHIFT = 60.0
STEEP = 1e20
BIG = 3.0e38


class Chain:

    def __init__(self, engine, sem):
        self.engine, self.sem, self.n = engine, sem, 0

    def post(self, instruction):
        self.n += 1
        instruction.then_inc(self.sem, 1)

    def wait(self):
        self.engine.wait_ge(self.sem, self.n)

    def run(self, instruction):
        self.post(instruction)
        self.wait()


class Tile:

    def __init__(self, k, c):
        self.k, self.c = k, c

    def __add__(self, n):
        return Tile(self.k, self.c + n)

    def count(self, n=0):
        return self.k * 4 + (self.c + n)

    def round(self, n=0):
        return self.k + (self.c // 4 + n)

    def known(self):
        return isinstance(self.k, int)

    def within(self, total):
        return not self.known() or 0 <= self.count() < total


def wait_from_first(engine, sem, value):
    if not isinstance(value, int) or value > 0:
        engine.wait_ge(sem, value)


def build(nc, x, adj, w, a, gamma, beta, gate_w, gate_b, w1, w2, w3, out):
    N, D = x.shape
    T = N // P
    HD = a.shape[0] // 2
    H = w.shape[1] // HD
    E, _, F = w1.shape
    C1 = HD + 1
    C2 = 2 * C1
    BLK = 2
    BT = T // BLK
    BW = BT * P
    Q = -(-(2 * T + E - 1) // 4) * 4
    RA = 2
    RZ = 4
    UNITS = BLK * T
    ON_DVE = [n for n in range(UNITS) if n % 5 == 4]
    ON_ACT = [n for n in range(UNITS) if n not in ON_DVE]
    FC = F // P

    xg = nc.dram_tensor("slot_inputs", (Q * P, D), F32, kind="Internal").ap()
    yg = nc.dram_tensor("slot_outputs", (Q * P, D), F32, kind="Internal").ap()
    x_v = x.rearrange("(t p) d -> p t d", p=P)
    out_v = out.rearrange("(t p) d -> p t d", p=P)

    ctx = ExitStack()
    with ctx:
        def sb(name, shape, dt=F32):
            return ctx.enter_context(nc.sbuf_tensor(name, shape, dt))

        def sem(name):
            return ctx.enter_context(nc.semaphore(name))

        R1 = sb("R1", [P, 8192])
        srcb = sb("srcb", [P, H, BLK, BW])
        maskT = sb("maskT", [P, T, N], BF16)
        feat = sb("feat", [P, H, T, 3, C2], BF16)
        ring = sb("ring", [P, 4096])
        S0 = sb("S0", [P, T, H, C1])
        S1 = sb("S1", [P, 4288])

        adj_t = [R1[:, N * r:N * (r + 1)] for r in range(RA)]
        mask_t = [R1[:, 4096 + 1024 * r:5120 + 1024 * r].bitcast(BF16) for r in range(2)]
        xnT = R1[:, 6144:8192]
        w12 = R1[:, :].rearrange("p (e f) -> p e f", e=E)
        step_t = [ring[:, 512 * r:512 * (r + 1)].bitcast(BF16) for r in range(RZ)]
        z_t = [ring[:, 2048 + 512 * r:2048 + 512 * (r + 1)].bitcast(BF16) for r in range(RZ)]
        xn = ring[:, 0:T * D].rearrange("p (t d) -> p t d", t=T)
        fd = ring[:, 0:T * H * C1].rearrange("p (t h c) -> p t h c", t=T, h=H)
        x_sb = S1[:, 0:T * D].rearrange("p (t d) -> p t d", t=T)
        fb = S1[:, 0:T * H * C1].rearrange("p (t h c) -> p t h c", t=T, h=H)
        HW = D + 2 * H
        hh = S1[:, T * H * C1:T * H * C1 + T * HW].rearrange("p (t c) -> p t c", t=T)
        s1 = S1[:, 0:H * T * C2].rearrange("p (h t c) -> p h t c", h=H, t=T)

        late = maskT[:, :, :].rearrange("p t n -> p (t n)").bitcast(F32)
        w3_sb = late[:, 0:4096].rearrange("p (e c o) -> p e c o", e=E, c=FC)

        def rows(k):
            return late[:, 4096 + 2048 * k:6144 + 2048 * k].rearrange("p (t d) -> p t d", t=T)
        x_again, x1, xn2, gat = rows(0), rows(1), rows(2), rows(3)
        xn2T = late[:, 12288:14336]
        tmp = late[:, 14336:16384].rearrange("p (t d) -> p t d", t=T)
        flat = srcb[:, :, :, :].rearrange("p h b n -> p (h b n)")
        xg_t = [flat[:, P * r:P * (r + 1)] for r in range(4)]
        xgT_t = [flat[:, 512 + P * r:512 + P * (r + 1)] for r in range(4)]
        y_t = [flat[:, 1024 + P * r:1024 + P * (r + 1)] for r in range(4)]
        silu_t = [flat[:, 1536 + F * r:1536 + F * (r + 1)] for r in range(2)]
        hid_t = [flat[:, 2048 + F * r:2048 + F * (r + 1)] for r in range(2)]
        hidT_t = [flat[:, 2560 + F * r:2560 + F * (r + 1)] for r in range(2)]
        y_pair = flat[:, 4096:8192].rearrange("p (t k d) -> p t k d", t=T, k=2)

        w_ext = sb("w_ext", [P, HW])
        wT = sb("wT", [P, P])
        a_blk = sb("a_blk", [P, 2 * H])
        w_src = sb("w_src", [P, H, P])
        ident = sb("ident", [P, P])
        ident_b = sb("ident_b", [P, P], BF16)
        gam = sb("gam", [P, D])
        bet = sb("bet", [P, D])
        gw = sb("gw", [P, E])
        gb = sb("gb", [P, E])
        stat = sb("stat", [P, T, 6])
        st1 = sb("st1", [P, T])
        st2 = sb("st2", [P, T])
        mean = sb("mean", [P, T])
        vare = sb("vare", [P, T])
        rstd = sb("rstd", [P, T])
        neg_half = sb("neg_half", [P, T])
        ones_f = sb("ones_f", [P, P])
        dloc = sb("dloc", [P, H])
        dmax = sb("dmax", [P, H])
        dn = sb("dn", [P, T, H])
        dnB = sb("dnB", [P, T, H])
        dnD = sb("dnD", [P, T, H])
        ndst = sb("ndst", [P, H, T])
        dsteep = sb("dsteep", [P, H, T])
        tt = sb("tt", [P, T, H])
        tmn = sb("tmn", [P, T, H])
        tmn2 = sb("tmn2", [P, T, H])
        eA = sb("eA", [P, T, H])
        eC = sb("eC", [P, T, H])
        rden = sb("rden", [P, T, H])
        zero = sb("zero", [P, D])
        before = sb("before", [P, P], BF16)
        ones_b = sb("ones_b", [P, P], BF16)
        first_e = sb("first_e", [P, E])
        lt_e = sb("lt_e", [P, E, E])
        k128 = sb("k128", [P, T])
        qrow = sb("qrow", [P, Q])

        banks = ctx.enter_context(nc.psum_tensor("banks", [P, 8, 512], F32))
        P8 = [banks[:, k, :] for k in range(8)]

        s_xld, s_wld, s_ald, s_gld = sem("x_loaded"), sem("w_loaded"), sem("a_loaded"), sem("gb_loaded")
        s_adj = [sem(f"adj_loaded{r}") for r in range(RA)]
        s_const = sem("constants_built")
        s_pool = sem("pool_steps")
        s_dve = sem("dve_steps")
        s_var = sem("variance_ready")
        s_rstd = sem("rstd_ready")
        s_xn = sem("xn_ready")
        s_tr = sem("transposes_done")
        s_xnT = sem("xnT_ready")
        s_wT = sem("wT_psum")
        s_wTs = sem("wT_sbuf")
        s_wa = sem("wa_psum")
        s_wext = sem("w_ext_ready")
        s_h = sem("h_psum")
        s_hs = sem("h_sbuf")
        s_src = sem("src_psum")
        s_srcs = sem("src_sbuf")
        s_dloc = sem("dloc_ready")
        s_dmax = sem("dmax_ready")
        s_dn = sem("exp_inputs_ready")
        s_exp = sem("exps_ready")
        s_fd = sem("fd_ready")
        s_fb = sem("fb_ready")
        s_mask = sem("mask_made")
        s_mtr = sem("mask_transposed")
        s_mT = sem("maskT_written")
        s_s0 = sem("s0_psum")
        s_s0f = sem("s0_evacuated")
        s_step = sem("step_made")
        s_turn = sem("step_turns")
        s_z = sem("z1_made")
        s_zu = sem("z1_used")
        s_acc = sem("acc_evacuated")
        s_w12 = sem("w12_loaded")
        s_w3 = sem("w3_loaded")
        s_zero = sem("slots_zeroed")
        s_lg = sem("logits_psum")
        s_M = sem("choices_made")
        s_rank = sem("ranks_psum")
        s_slot = sem("slots_ready")
        s_w2e = sem("second_exp")
        s_m2 = sem("second_exp_input")
        s_sc = sem("rows_scattered")
        s_xg = [sem(f"slot_tile_loaded{r}") for r in range(4)]
        s_t1 = sem("xg_transposed")
        s_xgT = sem("xgT_sbuf")
        s_hp = sem("hidden_psum")
        s_si = sem("silu_ready")
        s_hid = sem("hidden_ready")
        s_t2 = sem("hidden_transposed")
        s_hT = sem("hiddenT_sbuf")
        s_y = sem("y_psum")
        s_ys = sem("y_sbuf")
        s_yst = [sem(f"y_stored{r}") for r in range(4)]
        s_gath = [sem(f"y_gathered{g}") for g in range(4)]
        s_eid = sem("tile_experts_ready")
        s_fin = sem("out_ready")
        s_out = sem("out_stored")

        def routing(k):
            return flat[:, 4096 + 256 * k:4096 + 256 * (k + 1)]
        lg, lg2, eq, M1, M2 = [routing(k).rearrange("p (t e) -> p t e", t=T) for k in range(5)]
        big3 = routing(5).rearrange("p (e k) -> p e k", e=E)
        tri = routing(6).rearrange("p (e f) -> p e f", e=E)
        cmpq = flat[0:1, 4096 + 2048:4096 + 2048 + Q * E].rearrange("p (q e) -> p q e", q=Q)
        m1 = sb("m1", [P, T])
        m2 = sb("m2", [P, T])
        key1 = sb("key1", [P, T])
        Mb = sb("Mb", [P, T, E], BF16)
        e2 = sb("e2", [P, T])
        wt1 = sb("wt1", [P, T])
        wt2 = sb("wt2", [P, T])
        cnt = sb("cnt", [P, E])
        ntile = sb("ntile", [P, E])
        base = sb("base", [P, E])
        endq = sb("endq", [P, E])
        slot_f = sb("slot_f", [P, 2, T])
        slot_i = sb("slot_i", [P, 2, T], I32)
        eid_f = sb("eid_f", [1, Q])
        eid = sb("eid", [1, Q], I32)

        block = ctx.enter_context(nc.Block())

        def cut(engine, chain, f, rows_h, first, done):
            part = [feat[:, :, :, k, first:first + C1].rearrange("p h t c -> p t h c") for k in range(3)]
            chain.run(engine.tensor_tensor(
                f[:, :, :, 0:HD], rows_h[:, :, 0:D].rearrange("p t (h c) -> p t h c", h=H),
                f[:, :, :, HD:C1].to_broadcast([P, T, H, HD]), ALU.mult))
            chain.run(engine.tensor_copy(part[0], f))
            chain.run(engine.tensor_tensor(f, f, part[0], ALU.subtract))
            chain.run(engine.tensor_copy(part[1], f))
            engine.tensor_tensor(part[2], f, part[1], ALU.subtract).then_inc(done, 1)

        def over_tiles(engine, step):
            for c in range(4):
                step(Tile(0, c))
            with engine.Fori(1, Q // 4) as k:
                for c in range(4):
                    step(Tile(k, c))
            for c in range(3):
                step(Tile(Q // 4, c))

        @block.sync
        def _(sp):
            sp.dma_start(x_sb, x_v).then_inc(s_xld, 16)
            sp.dma_start(w_ext[:, 0:D], w).then_inc(s_wld, 16)
            for r in range(RA):
                sp.dma_start(adj_t[r], adj[P * r:P * (r + 1), :]).then_inc(s_adj[r], 16)
            with sp.Fori(1, T // RA) as k:
                for r in range(RA):
                    sp.wait_ge(s_mask, k * RA + (r + 1 - RA))
                    sp.dma_start(adj_t[r], adj[bass.ds(k * (RA * P) + P * r, P), :]).then_inc(s_adj[r], 16)
            sp.wait_ge(s_mtr, T)
            sp.wait_ge(s_src, H * 4)
            sp.dma_start(w12[:, :, 0:F], w1.rearrange("e d f -> d e f")).then_inc(s_w12, 16)
            sp.dma_start(w12[:, :, F:2 * F], w2.rearrange("e d f -> d e f")).then_inc(s_w12, 16)
            sp.wait_ge(s_zu, H * UNITS)
            sp.wait_ge(s_z, H * UNITS)
            sp.dma_start(x_again, x_v).then_inc(s_xld, 16)
            sp.dma_start(w3_sb, w3.rearrange("e (c p) o -> p e c o", p=P)).then_inc(s_w3, 16)
            sp.wait_ge(s_sc, 16 * 2 * T)
            for r in range(4):
                sp.dma_start(xg_t[r], xg[P * r:P * (r + 1), :]).then_inc(s_xg[r], 16)
            with sp.Fori(1, Q // 4) as k:
                for r in range(4):
                    sp.wait_ge(s_t1, k * 4 + (r - 3))
                    sp.dma_start(xg_t[r], xg[bass.ds(k * (4 * P) + P * r, P), :]).then_inc(s_xg[r], 16)
            for g in range(4):
                n = T // 4
                sp.wait_ge(s_fin, n * (g + 1))
                sp.dma_start(out_v[:, n * g:n * (g + 1), :], tmp[:, n * g:n * (g + 1), :]).then_inc(s_out, 16)
            sp.wait_ge(s_out, 64)

        @block.gpsimd
        def _(pool):
            g = nc.gpsimd
            chain = Chain(pool, s_pool)
            for tile, value in ((a_blk, 0.0), (ident, 0.0), (before, 1.0), (ones_b, 1.0), (ones_f, 1.0),
                                (zero, 0.0), (neg_half, -0.5), (lt_e, 1.0)):
                chain.post(g.memset(tile[:], value))
            chain.wait()
            for h in range(H):
                for side in range(2):
                    pool.dma_start(a_blk[HD * h:HD * (h + 1), side * H + h:side * H + h + 1],
                                   a[HD * side:HD * (side + 1), :]).then_inc(s_ald, 16)
            chain.post(g.affine_select(out=before[:], in_=before[:], compare_op=ALU.is_gt, fill=0.0, base=0,
                                       pattern=[[1, P]], channel_multiplier=-1))
            chain.post(g.affine_select(out=lt_e[:], in_=lt_e[:], compare_op=ALU.is_gt, fill=0.0, base=0,
                                       pattern=[[1, E], [-1, E]], channel_multiplier=0))
            for tile, step, count, first in ((first_e, -1, E, E), (k128, P, T, 0), (qrow, P, Q, 0)):
                chain.post(g.iota(tile[:], pattern=[[step, count]], base=first, channel_multiplier=0,
                                  allow_small_or_imprecise_dtypes=True))
            chain.run(g.affine_select(out=ident[:], in_=ident[:], compare_op=ALU.not_equal, fill=1.0, base=0,
                                      pattern=[[-1, P]], channel_multiplier=1))
            g.tensor_copy(ident_b[:], ident[:]).then_inc(s_const, 1)
            pool.dma_start(xg.rearrange("(q p) d -> p q d", p=P),
                           zero[:, :].unsqueeze(1).to_broadcast([P, Q, D])).then_inc(s_zero, 16)
            for dst, src in ((gam, gamma), (bet, beta), (gb, gate_b)):
                pool.dma_start(dst[:], src.partition_broadcast(P)).then_inc(s_gld, 16)
            pool.dma_start(gw[:], gate_w).then_inc(s_gld, 16)

            def root(k):
                pool.wait_ge(s_var, k)
                g.tensor_tensor(rstd[:], vare[:], neg_half[:], ALU.pow).then_inc(s_rstd, 1)

            root(1)
            pool.wait_ge(s_dloc, 1)
            g.partition_all_reduce(dmax[:], dloc[:], P, bass.bass_isa.ReduceOp.max).then_inc(s_dmax, 1)
            pool.wait_ge(s_exp, 2)
            pool.wait_ge(s_hs, 6)
            cut(g, chain, fb, hh, 0, s_fb)
            root(2)
            root(3)
            pool.wait_ge(s_slot, 1)
            pool.wait_ge(s_zero, 16)
            for t in range(T):
                for k in range(2):
                    g.indirect_dma_start(
                        out=xg, out_offset=bass.IndirectOffsetOnAxis(ap=slot_i[:, k, t:t + 1], axis=0),
                        in_=xn2[:, t, :], in_offset=None).then_inc(s_sc, 16)

            def store(tile):
                pool.wait_ge(s_ys, tile.count(1))
                rows_of = yg[P * tile.count():P * tile.count(1), :] if tile.known() else \
                    yg[bass.ds(tile.count() * P, P), :]
                pool.dma_start(rows_of, y_t[tile.c % 4]).then_inc(s_yst[tile.c % 4], 16)

            with pool.Fori(0, Q // 4) as k:
                for c in range(4):
                    store(Tile(k, c))
            for r in range(4):
                pool.wait_ge(s_yst[r], 16 * (Q // 4))
            for t in range(T):
                for k in range(2):
                    g.indirect_dma_start(
                        out=y_pair[:, t, k, :], out_offset=None, in_=yg,
                        in_offset=bass.IndirectOffsetOnAxis(ap=slot_i[:, k, t:t + 1], axis=0),
                    ).then_inc(s_gath[t // (T // 4)], 16)

        @block.scalar
        def _(act):
            s = nc.scalar
            for g in range(4):
                act.wait_ge(s_tr, g + 1)
                s.copy(xnT[:, 512 * g:512 * (g + 1)], P8[g][:, :]).then_inc(s_xnT, 1)
            act.wait_ge(s_dn, 1)
            s.activation(fd[:, :, :, HD], dnD[:, :, :], ACT.Exp).then_inc(s_exp, 1)
            act.wait_ge(s_dn, 2)
            s.activation(fb[:, :, :, HD], dnB[:, :, :], ACT.Exp).then_inc(s_exp, 1)
            act.wait_ge(s_dn, 4)
            s.activation(eA[:], tmn[:], ACT.Exp).then_inc(s_exp, 1)
            s.activation(eC[:], tmn2[:], ACT.Exp).then_inc(s_exp, 1)
            for n in range(4 * H):
                h, c = divmod(n, 4)
                act.wait_ge(s_src, n + 1)
                s.copy(srcb[:, h, c // 2, 512 * (c % 2):512 * (c % 2) + 512], P8[n % 4][:, :]).then_inc(s_srcs, 1)

            with act.Fori(0, T // 2) as k:
                for r in range(2):
                    act.wait_ge(s_mtr, k * 2 + (r + 1))
                    s.copy(maskT[:, :, bass.ds(k * (2 * P) + P * r, P)],
                           banks[:, 2 * r:2 * r + 2, :].rearrange("p b n -> p (b n)").bitcast(BF16)
                           .rearrange("p (j i) -> p j i", j=T)).then_inc(s_mT, 1)


            def steps(h, first):
                for j, n in enumerate(ON_ACT):
                    blk, jt = divmod(n, T)
                    if j >= RZ:
                        act.wait_ge(s_z, h * UNITS + (ON_ACT[j - RZ] + 1))
                    elif not first:
                        last = max(m for m in range(len(ON_ACT)) if m % RZ == j)
                        act.wait_ge(s_z, h * UNITS + (ON_ACT[last] + 1 - UNITS))
                    else:
                        act.wait_ge(s_fd, 1)
                    src_row = srcb[:, h, blk, :] if first else srcb[:, bass.ds(h, 1), blk, :].rearrange("p a n -> p (a n)")
                    bias = dsteep[:, h, jt:jt + 1] if first else dsteep[:, bass.ds(h, 1), jt]
                    if not first:
                        act.sem_inc(s_turn, 1)
                    s.activation(step_t[j % RZ], src_row, ACT.Sigmoid, bias=bias, scale=STEEP).then_inc(s_step, 1)

            act.wait_ge(s_srcs, 4 * H)
            steps(0, True)
            with act.Fori(1, H) as h:
                steps(h, False)

            for g in range(4):
                act.wait_ge(s_tr, 4 + g + 1)
                s.copy(xn2T[:, 512 * g:512 * (g + 1)], P8[g][:, :]).then_inc(s_xnT, 1)
            act.wait_ge(s_m2, 1)
            s.activation(e2[:], e2[:], ACT.Exp).then_inc(s_w2e, 1)

            def expert_step(tile):
                p = tile + -1
                if p.within(Q):
                    act.wait_ge(s_hp, p.count(1))
                    wait_from_first(act, s_hid, p.count(-1))
                    s.activation(silu_t[p.c % 2], P8[2 + p.c % 2][:, 0:F], ACT.Silu).then_inc(s_si, 1)
                p = tile + -2
                if p.within(Q):
                    act.wait_ge(s_t2, p.count(1))
                    wait_from_first(act, s_y, p.count(-1))
                    s.copy(hidT_t[p.c % 2], P8[4 + p.c % 2][:, 0:F]).then_inc(s_hT, 1)
            over_tiles(act, expert_step)

        @block.vector
        def _(dve):
            v = nc.vector
            chain = Chain(dve, s_dve)
            run, post = chain.run, chain.post

            def norm_stats(rows_in):
                for t in range(T):
                    post(v.bn_stats(stat[:, t, :], rows_in[:, t, :]))
                chain.wait()
                post(v.tensor_tensor(mean[:], stat[:, :, 1], stat[:, :, 4], ALU.add))
                post(v.tensor_tensor(st1[:], stat[:, :, 1], stat[:, :, 4], ALU.subtract))
                post(v.tensor_tensor(st2[:], stat[:, :, 2], stat[:, :, 5], ALU.add))
                chain.wait()
                post(v.tensor_scalar(mean[:], mean[:], 0.5, None, ALU.mult))
                post(v.tensor_tensor(st1[:], st1[:], st1[:], ALU.mult))
                post(v.tensor_scalar(st2[:], st2[:], 1.0 / D, EPS, ALU.mult, ALU.add))
                chain.wait()
                v.scalar_tensor_tensor(vare[:], st1[:], 0.25, st2[:], ALU.mult, ALU.add).then_inc(s_var, 1)

            def normalise(rows_out, rows_in, k):
                dve.wait_ge(s_rstd, k)
                for t in range(T):
                    post(v.tensor_scalar(rows_out[:, t, :], rows_in[:, t, :], mean[:, t:t + 1], rstd[:, t:t + 1],
                                         ALU.subtract, ALU.mult))
                chain.wait()

            dve.wait_ge(s_xld, 16)
            norm_stats(x_sb)
            dve.wait_ge(s_rstd, 1)
            for t in range(T):
                v.tensor_scalar(xn[:, t, :], x_sb[:, t, :], mean[:, t:t + 1], rstd[:, t:t + 1],
                                ALU.subtract, ALU.mult).then_inc(s_xn, 1)
            dve.wait_ge(s_wT, 1)
            v.tensor_copy(wT[:], P8[4][:, 0:P]).then_inc(s_wTs, 1)
            dve.wait_ge(s_wa, 1)
            run(v.tensor_copy(w_ext[:, D:HW], P8[5][:, 0:2 * H]))
            for h in range(H):
                v.tensor_scalar(w_src[:, h, :], ones_f[:], w_ext[:, D + h:D + h + 1], None, ALU.mult).then_inc(s_wext, 1)
            for g in range(6):
                n = min(3, T - 3 * g)
                dve.wait_ge(s_h, g + 1)
                v.tensor_copy(hh[:, 3 * g:3 * g + n, :],
                              P8[6 + g % 2][:, 0:n * HW].rearrange("p (t c) -> p t c", t=n)).then_inc(s_hs, 1)
            dve.wait_ge(s_hs, 6)
            src, dst = hh[:, :, D:D + H], hh[:, :, D + H:HW]
            v.tensor_reduce(dloc[:], dst.rearrange("p t h -> p h t"), AX.X, ALU.max).then_inc(s_dloc, 1)
            post(v.tensor_scalar(ndst[:].rearrange("p h t -> p t h"), dst, -1.0, None, ALU.mult))
            post(v.tensor_scalar(dsteep[:].rearrange("p h t -> p t h"), dst, STEEP, None, ALU.mult))
            dve.wait_ge(s_dmax, 1)
            dmax_b = dmax[:, :].unsqueeze(1).to_broadcast([P, T, H])
            post(v.tensor_tensor(dn[:], dst, dmax_b, ALU.subtract))
            post(v.tensor_tensor(tt[:], src, dmax_b, ALU.add))
            chain.wait()
            v.tensor_scalar(dnD[:], dn[:], 0.2, SHIFT, ALU.mult, ALU.add).then_inc(s_dn, 1)
            v.tensor_scalar(dnB[:], dn[:], SHIFT, None, ALU.add).then_inc(s_dn, 1)
            v.tensor_scalar(tmn[:], tt[:], 0.8, 0.0, ALU.mult, ALU.min).then_inc(s_dn, 1)
            v.tensor_scalar(tmn2[:], tt[:], -0.8, 0.0, ALU.mult, ALU.min).then_inc(s_dn, 1)
            dve.wait_ge(s_exp, 1)
            cut(v, chain, fd, hh, C1, s_fd)

            def mask(r):
                v.tensor_scalar(mask_t[r], adj_t[r], 0.0, None, ALU.is_gt).then_inc(s_mask, 1)

            def s0_sum(r, to):
                v.tensor_reduce(to, P8[4 + r][:, 0:3 * H * C1].rearrange("p (h k c) -> p h c k", h=H, k=3),
                                AX.X, ALU.add).then_inc(s_s0f, 1)

            for r in range(2):
                dve.wait_ge(s_adj[r], 16)
                mask(r)
            with dve.Fori(1, T // 2) as k:
                for r in range(2):
                    dve.wait_ge(s_adj[r], k * 16 + 16)
                    dve.wait_ge(s_mtr, k * 2 + (r - 1))
                    mask(r)
                    dve.wait_ge(s_s0, k * 2 + (r - 1))
                    s0_sum(r, S0[:, bass.ds(k * 2 + (r - 2), 1), :, :].rearrange("p a h c -> p (a h) c"))
            for r in range(2):
                dve.wait_ge(s_s0, T - 1 + r)
                s0_sum(r, S0[:, T - 2 + r, :, :])

            def z1(h, first):
                for n in range(UNITS):
                    blk, jt = divmod(n, T)
                    if not first or n >= RZ:
                        dve.wait_ge(s_zu, h * UNITS + (n + 1 - RZ))
                    z0 = maskT[:, jt, BW * blk:BW * (blk + 1)]
                    if n in ON_DVE:
                        src_row = srcb[:, h, blk, :] if first else \
                            srcb[:, bass.ds(h, 1), blk, :].rearrange("p a n -> p (a n)")
                        nd = ndst[:, h, jt:jt + 1] if first else ndst[:, bass.ds(h, 1), jt]
                        v.scalar_tensor_tensor(z_t[n % RZ], src_row, nd, z0, ALU.is_gt, ALU.mult).then_inc(s_z, 1)
                    else:
                        j = ON_ACT.index(n)
                        dve.wait_ge(s_step, h * len(ON_ACT) + (j + 1))
                        v.tensor_tensor(z_t[n % RZ], step_t[j % RZ], z0, ALU.mult).then_inc(s_z, 1)
                    if n == T + 2:
                        s1_sum(h, 0, h, first)
                    if n == 2 and not first:
                        s1_sum(h, 1, h - 1, False)

            def s1_sum(h, blk, hp, known):
                for b in range(4):
                    dve.wait_ge(s_zu, hp * UNITS + T * (blk + 1))
                    it = BT * blk + 2 * b
                    to = s1[:, hp, it:it + 2, :] if known else \
                        s1[:, bass.ds(hp, 1), it:it + 2, :].rearrange("p a i c -> p (a i) c")
                    v.tensor_reduce(to, P8[4 * blk + b][:, 0:6 * C2].rearrange("p (i k c) -> p i c k", i=2, k=3),
                                    AX.X, ALU.add).then_inc(s_acc, 1)

            dve.wait_ge(s_srcs, 4 * H)
            dve.wait_ge(s_mT, T)
            dve.wait_ge(s_fd, 1)
            dve.wait_ge(s_fb, 1)
            z1(0, True)
            with dve.Fori(1, H) as h:
                z1(h, False)
            s1_sum(H, 1, H - 1, True)
            dve.wait_ge(s_acc, 8 * H)
            dve.wait_ge(s_s0f, T)

            dve.wait_ge(s_exp, 4)
            s1B = s1[:, :, :, 0:C1].rearrange("p h t c -> p t h c")
            s1D = s1[:, :, :, C1:C2].rearrange("p h t c -> p t h c")
            post(v.tensor_tensor(S0[:], S0[:], s1D, ALU.subtract))
            post(v.tensor_tensor(s1B, s1B, eA[:].unsqueeze(3).to_broadcast([P, T, H, C1]), ALU.mult))
            chain.wait()
            run(v.tensor_tensor(S0[:], S0[:], eC[:].unsqueeze(3).to_broadcast([P, T, H, C1]), ALU.mult))
            run(v.tensor_tensor(S0[:], S0[:], s1B, ALU.add))
            run(v.reciprocal(rden[:], S0[:, :, :, HD]))
            run(v.tensor_tensor(gat.rearrange("p t (h c) -> p t h c", h=H), S0[:, :, :, 0:HD],
                                rden[:].unsqueeze(3).to_broadcast([P, T, H, HD]), ALU.mult))
            norm_stats(gat)
            normalise(tmp, gat, 2)
            dve.wait_ge(s_gld, 64)
            run(v.tensor_tensor(tmp, tmp, gam[:, :].unsqueeze(1).to_broadcast([P, T, D]), ALU.mult))
            run(v.tensor_tensor(tmp, tmp, bet[:, :].unsqueeze(1).to_broadcast([P, T, D]), ALU.add))
            dve.wait_ge(s_xld, 32)
            run(v.tensor_tensor(x1, tmp, x_again, ALU.add))
            norm_stats(x1)
            dve.wait_ge(s_rstd, 3)
            for t in range(T):
                v.tensor_scalar(xn2[:, t, :], x1[:, t, :], mean[:, t:t + 1], rstd[:, t:t + 1],
                                ALU.subtract, ALU.mult).then_inc(s_xn, 1)

            dve.wait_ge(s_lg, 1)
            run(v.tensor_tensor(lg, P8[4][:, 0:T * E].rearrange("p (t e) -> p t e", t=T),
                                gb[:, :].unsqueeze(1).to_broadcast([P, T, E]), ALU.add))

            def over_e(one_per_token):
                return one_per_token[:, :].unsqueeze(2).to_broadcast([P, T, E])
            order = first_e[:, :].unsqueeze(1).to_broadcast([P, T, E])

            def choose(logits, top, chosen):
                run(v.tensor_reduce(top[:], logits, AX.X, ALU.max))
                run(v.tensor_tensor(eq, logits, over_e(top), ALU.is_equal))
                run(v.tensor_tensor(eq, eq, order, ALU.mult))
                run(v.tensor_reduce(key1[:], eq, AX.X, ALU.max))
                run(v.tensor_tensor(chosen, order, over_e(key1), ALU.is_equal))
            choose(lg, m1, M1)
            run(v.scalar_tensor_tensor(lg2, M1, -BIG, lg, ALU.mult, ALU.add))
            choose(lg2, m2, M2)
            v.tensor_tensor(Mb[:], M1, M2, ALU.add).then_inc(s_M, 1)
            v.tensor_tensor(e2[:], m2[:], m1[:], ALU.subtract).then_inc(s_m2, 1)
            dve.wait_ge(s_rank, 2)
            run(v.tensor_copy(cnt[:], P8[6][:, 0:E]))
            run(v.tensor_tensor(big3, cnt[:, :].unsqueeze(2).to_broadcast([P, E, T]),
                                k128[:, :].unsqueeze(1).to_broadcast([P, E, T]), ALU.is_gt))
            run(v.tensor_reduce(ntile[:], big3, AX.X, ALU.add))
            run(v.tensor_tensor(tri, lt_e[:], ntile[:, :].unsqueeze(1).to_broadcast([P, E, E]), ALU.mult))
            run(v.tensor_reduce(base[:], tri, AX.X, ALU.add))
            run(v.tensor_tensor(endq[:], base[:], ntile[:], ALU.add))
            post(v.tensor_scalar(base[:], base[:], float(P), None, ALU.mult))
            post(v.tensor_scalar(endq[:], endq[:], float(P), None, ALU.mult))
            chain.wait()
            run(v.tensor_tensor(eq, P8[5][:, 0:T * E].rearrange("p (t e) -> p t e", t=T),
                                base[:, :].unsqueeze(1).to_broadcast([P, T, E]), ALU.add))
            post(v.tensor_tensor(M1, M1, eq, ALU.mult))
            post(v.tensor_tensor(M2, M2, eq, ALU.mult))
            chain.wait()
            post(v.tensor_reduce(slot_f[:, 0, :], M1, AX.X, ALU.add))
            post(v.tensor_reduce(slot_f[:, 1, :], M2, AX.X, ALU.add))
            chain.wait()
            v.tensor_copy(slot_i[:], slot_f[:]).then_inc(s_slot, 1)
            run(v.tensor_tensor(cmpq, endq[0:1, :].unsqueeze(1).to_broadcast([1, Q, E]),
                                qrow[0:1, :].unsqueeze(2).to_broadcast([1, Q, E]), ALU.is_le))
            run(v.tensor_reduce(eid_f[:], cmpq, AX.X, ALU.add))
            run(v.tensor_scalar(eid_f[:], eid_f[:], float(E - 1), None, ALU.min))
            v.tensor_copy(eid[:], eid_f[:]).then_inc(s_eid, 1)
            dve.wait_ge(s_w2e, 1)
            run(v.tensor_scalar(wt2[:], e2[:], 1.0, None, ALU.add))
            run(v.reciprocal(wt1[:], wt2[:]))
            run(v.tensor_tensor(wt2[:], e2[:], wt1[:], ALU.mult))

            def expert_step(tile):
                if tile.within(Q):
                    dve.wait_ge(s_t1, tile.count(1))
                    wait_from_first(dve, s_hp, tile.count(-3))
                    v.tensor_copy(xgT_t[tile.c % 4], P8[tile.c % 2][:, 0:P]).then_inc(s_xgT, 1)
                p = tile + -1
                if p.within(Q):
                    dve.wait_ge(s_si, p.count(1))
                    wait_from_first(dve, s_t2, p.count(-1))
                    v.tensor_tensor(hid_t[p.c % 2], silu_t[p.c % 2], P8[2 + p.c % 2][:, F:2 * F],
                                    ALU.mult).then_inc(s_hid, 1)
                p = tile + -3
                if p.within(Q):
                    dve.wait_ge(s_y, p.count(1))
                    wait_from_first(dve, s_yst[p.c % 4], p.round() * 16)
                    v.tensor_copy(y_t[p.c % 4], P8[6 + p.c % 2][:, 0:D]).then_inc(s_ys, 1)
            over_tiles(dve, expert_step)

            n = T // 4
            for g in range(4):
                dve.wait_ge(s_gath[g], 16 * 2 * n)
                for t in range(n * g, n * (g + 1)):
                    post(v.scalar_tensor_tensor(tmp[:, t, :], y_pair[:, t, 0, :], wt1[:, t:t + 1], x1[:, t, :],
                                                ALU.mult, ALU.add))
                chain.wait()
                for t in range(n * g, n * (g + 1)):
                    v.scalar_tensor_tensor(tmp[:, t, :], y_pair[:, t, 1, :], wt2[:, t:t + 1], tmp[:, t, :],
                                           ALU.mult, ALU.add).then_inc(s_fin, 1)

        @block.tensor
        def _(pe):
            mm, tp = nc.tensor.matmul, nc.tensor.transpose
            pe.wait_ge(s_wld, 16)
            pe.wait_ge(s_const, 1)
            tp(P8[4][:, 0:P], w_ext[:, 0:D], ident[:]).then_inc(s_wT, 1)
            pe.wait_ge(s_wTs, 1)
            pe.wait_ge(s_ald, 16 * 2 * H)
            mm(P8[5][:, 0:2 * H], wT[:], a_blk[:], start=True, stop=True).then_inc(s_wa, 1)
            for g in range(4):
                pe.wait_ge(s_xn, 4 * (g + 1))
                for t in range(4):
                    last = tp(P8[g][:, P * t:P * (t + 1)], xn[:, 4 * g + t, :], ident[:])
                last.then_inc(s_tr, 1)
            pe.wait_ge(s_xnT, 4)
            pe.wait_ge(s_wext, H)
            for g in range(6):
                if g >= 2:
                    pe.wait_ge(s_hs, g - 1)
                for t in range(3 * g, min(3 * g + 3, T)):
                    last = mm(P8[6 + g % 2][:, HW * (t - 3 * g):HW * (t - 3 * g + 1)], xnT[:, P * t:P * (t + 1)],
                              w_ext[:, :], start=True, stop=True)
                last.then_inc(s_h, 1)
            for n in range(4 * H):
                h, c = divmod(n, 4)
                if n >= 4:
                    pe.wait_ge(s_srcs, n - 3)
                mm(P8[n % 4][:, :], w_src[:, h, :], xnT[:, 512 * c:512 * (c + 1)], start=True, stop=True
                   ).then_inc(s_src, 1)
            pe.wait_ge(s_srcs, 4 * H)

            def transpose_mask(r):
                for j in range(T):
                    last = tp(P8[2 * r + j // 8][:, 64 * (j % 8):64 * (j % 8 + 1)].bitcast(BF16),
                              mask_t[r][:, P * j:P * (j + 1)], ident_b[:])
                last.then_inc(s_mtr, 1)

            def s0_products(r, rows_of):
                for j in range(T):
                    last = mm(P8[4 + r][:, 0:3 * H * C1], maskT[:, j, rows_of],
                              feat[:, :, j, :, C1:C2], start=(j == 0), stop=(j == T - 1))
                last.then_inc(s_s0, 1)

            for r in range(2):
                pe.wait_ge(s_mask, r + 1)
                transpose_mask(r)
                if r == 1:
                    pe.wait_ge(s_mT, 1)
                    pe.wait_ge(s_fd, 1)
                    s0_products(0, slice(0, P))
            with pe.Fori(1, T // 2) as k:
                for r in range(2):
                    pe.wait_ge(s_mask, k * 2 + (r + 1))
                    pe.wait_ge(s_mT, k * 2 + (r - 1))
                    transpose_mask(r)
                    pe.wait_ge(s_mT, k * 2 + r)
                    pe.wait_ge(s_s0f, k * 2 + (r - 2))
                    if r == 1:
                        s0_products(0, bass.ds(k * (2 * P), P))
                    else:
                        s0_products(1, bass.ds(k * (2 * P) - P, P))
            pe.wait_ge(s_mT, T)
            pe.wait_ge(s_s0f, T - 2)
            s0_products(1, slice(P * (T - 1), P * T))

            def z1_products(h, first):
                for n in range(UNITS):
                    blk, jt = divmod(n, T)
                    pe.wait_ge(s_z, h * UNITS + (n + 1))
                    moving = feat[:, h, jt, :, :].rearrange("p k c -> p (k c)") if first else \
                        feat[:, bass.ds(h, 1), jt, :, :].rearrange("p a k c -> p (a k c)")
                    for i in range(BT):
                        b = 4 * blk + i // 2
                        if jt == 0 and i % 2 == 0 and not first:
                            pe.wait_ge(s_acc, h * 8 + (b + 1 - 8))
                        last = mm(P8[b][:, 3 * C2 * (i % 2):3 * C2 * (i % 2 + 1)], z_t[n % RZ][:, P * i:P * (i + 1)],
                                  moving, start=(jt == 0 and i % 2 == 0), stop=(jt == T - 1), skip_group_check=True)
                    last.then_inc(s_zu, 1)
            pe.wait_ge(s_s0f, T)
            pe.wait_ge(s_fb, 1)
            z1_products(0, True)
            with pe.Fori(1, H) as h:
                z1_products(h, False)

            pe.wait_ge(s_acc, 8 * H)
            for g in range(4):
                pe.wait_ge(s_xn, T + 4 * (g + 1))
                for t in range(4):
                    last = tp(P8[g][:, P * t:P * (t + 1)], xn2[:, 4 * g + t, :], ident[:])
                last.then_inc(s_tr, 1)
            pe.wait_ge(s_xnT, 8)
            pe.wait_ge(s_gld, 64)
            for t in range(T):
                last = mm(P8[4][:, E * t:E * (t + 1)], xn2T[:, P * t:P * (t + 1)], gw[:], start=True, stop=True)
            last.then_inc(s_lg, 1)
            pe.wait_ge(s_M, 1)
            mm(P8[5][:, 0:T * E], before[:], Mb[:, :, :].rearrange("p t e -> p (t e)"), start=True, stop=False)
            for t in range(T - 1):
                last = mm(P8[5][:, E * (t + 1):T * E].rearrange("p (t e) -> p t e", e=E), ones_b[:],
                          Mb[:, t:t + 1, :].to_broadcast([P, T - 1 - t, E]), start=False, stop=(t == T - 2))
            last.then_inc(s_rank, 1)
            for t in range(T):
                last = mm(P8[6][:, 0:E], ones_b[:], Mb[:, t, :], start=(t == 0), stop=(t == T - 1))
            last.then_inc(s_rank, 1)

            pe.wait_ge(s_w12, 32)
            pe.wait_ge(s_w3, 16)
            pe.wait_ge(s_eid, 1)

            def expert_of(p):
                at = slice(p.count(), p.count(1)) if p.known() else bass.ds(p.count(), 1)
                return pe.value_load(eid[0:1, at], min_val=0, max_val=E - 1)

            def expert_step(tile):
                if tile.within(Q):
                    r = tile.c % 4
                    pe.wait_ge(s_xg[r], tile.round(1) * 16)
                    wait_from_first(pe, s_xgT, tile.count(-1))
                    tp(P8[tile.c % 2][:, 0:P], xg_t[r], ident[:]).then_inc(s_t1, 1)
                p = tile + -1
                if p.within(Q):
                    e = expert_of(p)
                    pe.wait_ge(s_xgT, p.count(1))
                    wait_from_first(pe, s_hid, p.count(-1))
                    mm(P8[2 + p.c % 2][:, :], xgT_t[p.c % 4], R1[:, bass.ds(e * (2 * F), 2 * F)],
                       start=True, stop=True).then_inc(s_hp, 1)
                p = tile + -2
                if p.within(Q):
                    pe.wait_ge(s_hid, p.count(1))
                    wait_from_first(pe, s_hT, p.count(-1))
                    for c in range(FC):
                        last = tp(P8[4 + p.c % 2][:, P * c:P * (c + 1)], hid_t[p.c % 2][:, P * c:P * (c + 1)], ident[:])
                    last.then_inc(s_t2, 1)
                p = tile + -3
                if p.within(Q):
                    e = expert_of(p)
                    pe.wait_ge(s_hT, p.count(1))
                    wait_from_first(pe, s_ys, p.count(-1))
                    for c in range(FC):
                        last = mm(P8[6 + p.c % 2][:, 0:D], hidT_t[p.c % 2][:, P * c:P * (c + 1)],
                                  late[:, bass.ds(e * (FC * D) + c * D, D)], start=(c == 0), stop=(c == FC - 1))
                    last.then_inc(s_y, 1)
            over_tiles(pe, expert_step)


_INS = ["x", "adj", "L0_gnn_W", "L0_gnn_a", "L0_gnn_gamma", "L0_gnn_beta", "L0_ffn_gate_w", "L0_ffn_gate_b",
        "L0_ffn_w1", "L0_ffn_w2", "L0_ffn_w3"]


def kernel(**inputs):
    import numpy as np
    import concourse.bacc as bacc
    from concourse.bass_utils import run_bass_kernel_spmd

    nc = bacc.Bacc("TRN2", target_bir_lowering=False, num_devices=1)
    arrays, args = {}, []
    for name in _INS:
        array = np.ascontiguousarray(inputs[name])
        arrays[name] = array
        args.append(nc.dram_tensor(name, array.shape, F32, kind="ExternalInput").ap())
    out = nc.dram_tensor("out", inputs["x"].shape, F32, kind="ExternalOutput").ap()
    build(nc, *args, out)
    got = run_bass_kernel_spmd(nc, [arrays], core_ids=[0])
    return got.results[0]["out"]
```

```python
from contextlib import ExitStack

import concourse.bass as bass
from concourse import mybir

F32 = mybir.dt.float32
BF16 = mybir.dt.bfloat16
I32 = mybir.dt.int32
ALU = mybir.AluOpType
ACT = mybir.ActivationFunctionType
AX = mybir.AxisListType

P = 128
EPS = 1e-5
SHIFT = 60.0
STEEP = 1e20
BIG = 3.0e38


class Chain:

    def __init__(self, engine, sem):
        self.engine, self.sem, self.n = engine, sem, 0

    def post(self, instruction):
        self.n += 1
        instruction.then_inc(self.sem, 1)

    def wait(self):
        self.engine.wait_ge(self.sem, self.n)

    def run(self, instruction):
        self.post(instruction)
        self.wait()


RING = 8


class Tile:

    def __init__(self, k, c):
        self.k, self.c = k, c

    def __add__(self, n):
        return Tile(self.k, self.c + n)

    def count(self, n=0):
        return self.k * RING + (self.c + n)

    def round(self, size, n=0):
        return self.k * (RING // size) + (self.c // size + n)

    def known(self):
        return isinstance(self.k, int)

    def within(self, total):
        return not self.known() or 0 <= self.count() < total


def wait_from_first(engine, sem, value):
    if not isinstance(value, int) or value > 0:
        engine.wait_ge(sem, value)


def build(nc, x, adj, w, a, gamma, beta, gate_w, gate_b, w1, w2, w3, out):
    N, D = x.shape
    T = N // P
    HD = a.shape[0] // 2
    H = w.shape[1] // HD
    E, _, F = w1.shape
    C1 = HD + 1
    C2 = 2 * C1
    BLK = 2
    BT = T // BLK
    BW = BT * P
    Q = -(-(2 * T + E - 1) // RING) * RING
    REGION = N + P
    ROW = D + 2
    RA = 2
    RZ = 4
    UNITS = BLK * T
    ON_DVE = [n for n in range(UNITS) if n % 5 == 4]
    ON_ACT = [n for n in range(UNITS) if n not in ON_DVE]
    FC = F // P

    xg = nc.dram_tensor("slots", (E * REGION, ROW), F32, kind="Internal").ap()
    yg = nc.dram_tensor("expert_rows", (2 * N, D), F32, kind="Internal").ap()
    yg_v = yg.rearrange("(t p k) d -> p t (k d)", k=2, p=P)
    x_v = x.rearrange("(t p) d -> p t d", p=P)
    out_v = out.rearrange("(t p) d -> p t d", p=P)

    ctx = ExitStack()
    with ctx:
        def sb(name, shape, dt=F32):
            return ctx.enter_context(nc.sbuf_tensor(name, shape, dt))

        def sem(name):
            return ctx.enter_context(nc.semaphore(name))

        R1 = sb("R1", [P, 8192])
        srcb = sb("srcb", [P, H, BLK, BW])
        maskT = sb("maskT", [P, T, N], BF16)
        feat = sb("feat", [P, H, T, 3, C2], BF16)
        ring = sb("ring", [P, 4096])
        S0 = sb("S0", [P, T, H, C1])
        S1 = sb("S1", [P, 4288])

        adj_t = [R1[:, N * r:N * (r + 1)] for r in range(RA)]
        mask_t = [R1[:, 4096 + 1024 * r:5120 + 1024 * r].bitcast(BF16) for r in range(2)]
        xnT = R1[:, 6144:8192]
        w12 = R1[:, :].rearrange("p (e f) -> p e f", e=E)
        step_t = [ring[:, 512 * r:512 * (r + 1)].bitcast(BF16) for r in range(RZ)]
        z_t = [ring[:, 2048 + 512 * r:2048 + 512 * (r + 1)].bitcast(BF16) for r in range(RZ)]
        xn = ring[:, 0:T * D].rearrange("p (t d) -> p t d", t=T)
        fd = ring[:, 0:T * H * C1].rearrange("p (t h c) -> p t h c", t=T, h=H)
        x_sb = S1[:, 0:T * D].rearrange("p (t d) -> p t d", t=T)
        fb = S1[:, 0:T * H * C1].rearrange("p (t h c) -> p t h c", t=T, h=H)
        HW = D + 2 * H
        hh = S1[:, T * H * C1:T * H * C1 + T * HW].rearrange("p (t c) -> p t c", t=T)
        s1 = S1[:, 0:H * T * C2].rearrange("p (h t c) -> p h t c", h=H, t=T)

        late = maskT[:, :, :].rearrange("p t n -> p (t n)").bitcast(F32)
        w3_sb = late[:, 0:4096].rearrange("p (e c o) -> p e c o", e=E, c=FC)

        def rows(k):
            return late[:, 4096 + 2048 * k:6144 + 2048 * k].rearrange("p (t d) -> p t d", t=T)
        x_again, x1, gat = rows(0), rows(1), rows(3)
        row_k = [S1[:, T * ROW * k:T * ROW * (k + 1)].rearrange("p (t c) -> p t c", t=T) for k in range(2)]
        xn2 = row_k[0][:, :, 0:D]
        xn2T = late[:, 12288:14336]
        tmp = late[:, 14336:16384].rearrange("p (t d) -> p t d", t=T)
        flat = srcb[:, :, :, :].rearrange("p h b n -> p (h b n)")
        xgT_t = [flat[:, P * r:P * (r + 1)] for r in range(4)]
        y_t = [flat[:, 512 + P * r:512 + P * (r + 1)] for r in range(4)]
        silu_t = [flat[:, 1024 + F * r:1024 + F * (r + 1)] for r in range(2)]
        hid_t = [flat[:, 1536 + F * r:1536 + F * (r + 1)] for r in range(2)]
        hidT_t = [flat[:, 2048 + F * r:2048 + F * (r + 1)] for r in range(2)]
        xg_t = [flat[:, 2560 + ROW * r:2560 + ROW * (r + 1)] for r in range(RING)]
        y_pair = flat[:, 4096:8192].rearrange("p (t c) -> p t c", t=T)

        w_ext = sb("w_ext", [P, HW])
        a_blk = sb("a_blk", [P, 2 * H])
        s0_flat = S0[:, :, :, :].rearrange("p t h c -> p (t h c)")
        w_src = s0_flat[:, 0:H * P].rearrange("p (h c) -> p h c", h=H)
        wT = s0_flat[:, H * P:(H + 1) * P]
        ones_f = s0_flat[:, (H + 1) * P:(H + 2) * P]
        ident = sb("ident", [P, P])
        ident_b = sb("ident_b", [P, P], BF16)
        gam = sb("gam", [P, D])
        bet = sb("bet", [P, D])
        gw = sb("gw", [P, E])
        gb = sb("gb", [P, E])
        stat = sb("stat", [P, T, 6])
        st1 = sb("st1", [P, T])
        st2 = sb("st2", [P, T])
        mean = sb("mean", [P, T])
        vare = sb("vare", [P, T])
        rstd = sb("rstd", [P, T])
        neg_half = sb("neg_half", [P, T])
        dloc = sb("dloc", [P, H])
        dmax = sb("dmax", [P, H])
        dn = sb("dn", [P, T, H])
        dnB = sb("dnB", [P, T, H])
        dnD = sb("dnD", [P, T, H])
        ndst = sb("ndst", [P, H, T])
        dsteep = sb("dsteep", [P, H, T])
        tt = sb("tt", [P, T, H])
        tmn = sb("tmn", [P, T, H])
        tmn2 = sb("tmn2", [P, T, H])
        eA = sb("eA", [P, T, H])
        eC = sb("eC", [P, T, H])
        rden = sb("rden", [P, T, H])
        pad_rows = sb("pad_rows", [P, ROW])
        before = sb("before", [P, P], BF16)
        ones_b = sb("ones_b", [P, P], BF16)
        first_e = sb("first_e", [P, E])
        lt_e = sb("lt_e", [P, E, E])
        k128 = sb("k128", [P, T])
        qtile = sb("qtile", [1, Q])
        region = sb("region", [P, E])
        e_row = sb("e_row", [1, E])
        goes_to = sb("goes_to", [P, 2, T], I32)

        banks = ctx.enter_context(nc.psum_tensor("banks", [P, 8, 512], F32))
        P8 = [banks[:, k, :] for k in range(8)]

        s_xld, s_wld, s_ald, s_gld = sem("x_loaded"), sem("w_loaded"), sem("a_loaded"), sem("gb_loaded")
        s_adj = [sem(f"adj_loaded{r}") for r in range(RA)]
        s_const = sem("constants_built")
        s_pool = sem("pool_steps")
        s_dve = sem("dve_steps")
        s_var = sem("variance_ready")
        s_rstd = sem("rstd_ready")
        s_xn = sem("xn_ready")
        s_tr = sem("transposes_done")
        s_xnT = sem("xnT_ready")
        s_wT = sem("wT_psum")
        s_wTs = sem("wT_sbuf")
        s_wa = sem("wa_psum")
        s_wext = sem("w_ext_ready")
        s_h = sem("h_psum")
        s_hs = sem("h_sbuf")
        s_src = sem("src_psum")
        s_srcs = sem("src_sbuf")
        s_dloc = sem("dloc_ready")
        s_dmax = sem("dmax_ready")
        s_dn = sem("exp_inputs_ready")
        s_exp = sem("exps_ready")
        s_fd = sem("fd_ready")
        s_fb = sem("fb_ready")
        s_mask = sem("mask_made")
        s_mtr = sem("mask_transposed")
        s_mT = sem("maskT_written")
        s_s0 = sem("s0_psum")
        s_s0f = sem("s0_evacuated")
        s_step = sem("step_made")
        s_turn = sem("step_turns")
        s_z = sem("z1_made")
        s_zu = sem("z1_used")
        s_acc = sem("acc_evacuated")
        s_w12 = sem("w12_loaded")
        s_w3 = sem("w3_loaded")
        s_pad = sem("slots_padded")
        s_pads = sem("pad_places_ready")
        s_rowA = sem("first_rows_columns")
        s_rowB = sem("second_rows_copied")
        s_rowC = sem("second_rows_columns")
        s_lg = sem("logits_psum")
        s_M = sem("choices_made")
        s_rank = sem("ranks_psum")
        s_slot = sem("slots_ready")
        s_w2e = sem("second_exp")
        s_m2 = sem("second_exp_input")
        s_sc = sem("rows_scattered")
        s_xg = [sem(f"slot_tile_loaded{r}") for r in range(RING)]
        s_turn2 = sem("scatter_turns")
        s_t1 = sem("xg_transposed")
        s_xgT = sem("xgT_sbuf")
        s_hp = sem("hidden_psum")
        s_si = sem("silu_ready")
        s_hid = sem("hidden_ready")
        s_t2 = sem("hidden_transposed")
        s_hT = sem("hiddenT_sbuf")
        s_y = sem("y_psum")
        s_ys = sem("y_sbuf")
        s_yst = [sem(f"y_stored{r}") for r in range(4)]
        s_gath = [sem(f"y_gathered{g}") for g in range(4)]
        s_eid = sem("tile_experts_ready")
        s_fin = sem("out_ready")
        s_out = sem("out_stored")

        def routing(k):
            return flat[:, 4096 + 256 * k:4096 + 256 * (k + 1)]
        lg, lg2, eq, M1, M2 = [routing(k).rearrange("p (t e) -> p t e", t=T) for k in range(5)]
        big3 = routing(5).rearrange("p (e k) -> p e k", e=E)
        tri = routing(6).rearrange("p (e f) -> p e f", e=E)
        cmpq = flat[0:1, 4096 + 2048:4096 + 2048 + Q * E].rearrange("p (q e) -> p q e", q=Q)
        hotq = flat[0:1, 4096 + 3072:4096 + 3072 + Q * E].rearrange("p (q e) -> p q e", q=Q)
        m1 = sb("m1", [P, T])
        m2 = sb("m2", [P, T])
        key1 = sb("key1", [P, T])
        Mb = sb("Mb", [P, T, E], BF16)
        e2 = sb("e2", [P, T])
        wt1 = sb("wt1", [P, T])
        wt2 = sb("wt2", [P, T])
        cnt = sb("cnt", [P, E])
        ntile = sb("ntile", [P, E])
        base = sb("base", [P, E])
        endq = sb("endq", [P, E])
        slot_f = sb("slot_f", [P, 2, T])
        slot_i = sb("slot_i", [P, 2, T], I32)
        eid_f = sb("eid_f", [1, Q])
        eid = sb("eid", [1, 4 + Q + 4], I32)
        at_f = sb("at_f", [1, Q])
        live = sb("live", [1, Q])
        place = sb("place", [1, Q], I32)
        off_e = sb("off_e", [1, E])
        pad_f = sb("pad_f", [1, E])
        pad_at = sb("pad_at", [1, E], I32)

        block = ctx.enter_context(nc.Block())

        def cut(engine, chain, f, rows_h, first, done):
            part = [feat[:, :, :, k, first:first + C1].rearrange("p h t c -> p t h c") for k in range(3)]
            chain.run(engine.tensor_tensor(
                f[:, :, :, 0:HD], rows_h[:, :, 0:D].rearrange("p t (h c) -> p t h c", h=H),
                f[:, :, :, HD:C1].to_broadcast([P, T, H, HD]), ALU.mult))
            chain.run(engine.tensor_copy(part[0], f))
            chain.run(engine.tensor_tensor(f, f, part[0], ALU.subtract))
            chain.run(engine.tensor_copy(part[1], f))
            engine.tensor_tensor(part[2], f, part[1], ALU.subtract).then_inc(done, 1)

        def over_tiles(engine, step):
            for c in range(RING):
                step(Tile(0, c))
            with engine.Fori(1, Q // RING) as k:
                for c in range(RING):
                    step(Tile(k, c))
            for c in range(3):
                step(Tile(Q // RING, c))

        @block.sync
        def _(sp):
            sp.dma_start(x_sb, x_v).then_inc(s_xld, 16)
            sp.dma_start(w_ext[:, 0:D], w).then_inc(s_wld, 16)
            for r in range(RA):
                sp.dma_start(adj_t[r], adj[P * r:P * (r + 1), :]).then_inc(s_adj[r], 16)
            with sp.Fori(1, T // RA) as k:
                for r in range(RA):
                    sp.wait_ge(s_mask, k * RA + (r + 1 - RA))
                    sp.dma_start(adj_t[r], adj[bass.ds(k * (RA * P) + P * r, P), :]).then_inc(s_adj[r], 16)
            sp.wait_ge(s_mtr, T)
            sp.wait_ge(s_src, H * 4)
            sp.dma_start(w12[:, :, 0:F], w1.rearrange("e d f -> d e f")).then_inc(s_w12, 16)
            sp.dma_start(w12[:, :, F:2 * F], w2.rearrange("e d f -> d e f")).then_inc(s_w12, 16)
            sp.wait_ge(s_zu, H * UNITS)
            sp.wait_ge(s_z, H * UNITS)
            sp.dma_start(x_again, x_v).then_inc(s_xld, 16)
            sp.dma_start(w3_sb, w3.rearrange("e (c p) o -> p e c o", p=P)).then_inc(s_w3, 16)
            sp.wait_ge(s_pads, 1)
            with sp.Fori(0, E) as e:
                at = sp.value_load(pad_at[0:1, bass.ds(e, 1)], min_val=0, max_val=E * REGION - P)
                sp.dma_start(xg[bass.ds(at, P), :], pad_rows[:]).then_inc(s_pad, 16)

            sp.wait_ge(s_eid, 1)
            sp.wait_ge(s_pad, 16 * E)
            sp.wait_ge(s_sc, 16 * 2 * T)

            def load_tile(tile):
                at = place[0:1, tile.c:tile.c + 1] if tile.known() else place[0:1, bass.ds(tile.count(), 1)]
                at = sp.value_load(at, min_val=0, max_val=E * REGION - P)
                if not tile.known():
                    sp.wait_ge(s_yst[tile.c % 4], tile.round(4, 1 - RING // 4) * 16)
                sp.dma_start(xg_t[tile.c % RING], xg[bass.ds(at, P), :]).then_inc(s_xg[tile.c % RING], 16)
            for c in range(RING):
                load_tile(Tile(0, c))
            with sp.Fori(1, Q // RING) as k:
                for c in range(RING):
                    load_tile(Tile(k, c))
            for r in range(4):
                sp.wait_ge(s_yst[r], 16 * (Q // 4))
            for g in range(4):
                n = T // 4
                sp.dma_start(y_pair[:, n * g:n * (g + 1), :], yg_v[:, n * g:n * (g + 1), :]).then_inc(s_gath[g], 16)
            for g in range(4):
                n = T // 4
                sp.wait_ge(s_fin, g + 1)
                sp.dma_start(out_v[:, n * g:n * (g + 1), :], tmp[:, n * g:n * (g + 1), :]).then_inc(s_out, 16)
            sp.wait_ge(s_out, 64)

        @block.gpsimd
        def _(pool):
            g = nc.gpsimd
            chain = Chain(pool, s_pool)
            for tile, value in ((a_blk, 0.0), (ident, 0.0), (before, 1.0), (ones_b, 1.0), (ones_f, 1.0),
                                (pad_rows, 0.0), (neg_half, -0.5), (lt_e, 1.0)):
                chain.post(g.memset(tile[:, :], value))
            chain.wait()
            for h in range(H):
                for side in range(2):
                    pool.dma_start(a_blk[HD * h:HD * (h + 1), side * H + h:side * H + h + 1],
                                   a[HD * side:HD * (side + 1), :]).then_inc(s_ald, 16)
            chain.post(g.affine_select(out=before[:], in_=before[:], compare_op=ALU.is_gt, fill=0.0, base=0,
                                       pattern=[[1, P]], channel_multiplier=-1))
            chain.post(g.affine_select(out=lt_e[:], in_=lt_e[:], compare_op=ALU.is_gt, fill=0.0, base=0,
                                       pattern=[[1, E], [-1, E]], channel_multiplier=0))
            for tile, step, count, first in ((first_e, -1, E, E), (k128, P, T, 0), (qtile, 1, Q, 0),
                                             (region, REGION, E, 0), (e_row, 1, E, 0)):
                chain.post(g.iota(tile[:], pattern=[[step, count]], base=first, channel_multiplier=0,
                                  allow_small_or_imprecise_dtypes=True))
            chain.run(g.affine_select(out=ident[:], in_=ident[:], compare_op=ALU.not_equal, fill=1.0, base=0,
                                      pattern=[[-1, P]], channel_multiplier=1))
            g.tensor_copy(ident_b[:], ident[:]).then_inc(s_const, 1)
            chain.post(g.iota(goes_to[:], pattern=[[1, 2], [2 * P, T]], base=0, channel_multiplier=2))
            chain.post(g.iota(pad_rows[:, D:D + 1].bitcast(I32), pattern=[[0, 1]], base=2 * N, channel_multiplier=0))
            chain.run(g.memset(eid[:], 0))
            for dst, src in ((gam, gamma), (bet, beta), (gb, gate_b)):
                pool.dma_start(dst[:], src.partition_broadcast(P)).then_inc(s_gld, 16)
            pool.dma_start(gw[:], gate_w).then_inc(s_gld, 16)

            def root(k):
                pool.wait_ge(s_var, k)
                g.tensor_tensor(rstd[:], vare[:], neg_half[:], ALU.pow).then_inc(s_rstd, 1)

            root(1)
            pool.wait_ge(s_dloc, 1)
            g.partition_all_reduce(dmax[:], dloc[:], P, bass.bass_isa.ReduceOp.max).then_inc(s_dmax, 1)
            pool.wait_ge(s_exp, 2)
            pool.wait_ge(s_hs, 6)
            cut(g, chain, fb, hh, 0, s_fb)
            root(2)
            root(3)
            pool.wait_ge(s_slot, 1)
            for k in range(2):
                if k == 0:
                    pool.wait_ge(s_xn, 2 * T)
                    pool.wait_ge(s_rowA, 2)
                else:
                    pool.wait_ge(s_rowB, 1)
                    pool.wait_ge(s_rowC, 2)
                for t in range(T):
                    g.indirect_dma_start(
                        out=xg, out_offset=bass.IndirectOffsetOnAxis(ap=slot_i[:, k, t:t + 1], axis=0),
                        in_=row_k[k][:, t, :], in_offset=None).then_inc(s_sc, 16)

            with pool.Fori(0, Q // RING) as k:
                for c in range(RING):
                    tile = Tile(k, c)
                    pool.wait_ge(s_ys, tile.count(1))
                    pool.sem_inc(s_turn2, 1)
                    g.indirect_dma_start(
                        out=yg, out_offset=bass.IndirectOffsetOnAxis(ap=xg_t[c][:, D:D + 1].bitcast(I32), axis=0),
                        in_=y_t[c % 4], in_offset=None, bounds_check=2 * N - 1, oob_is_err=False,
                    ).then_inc(s_yst[c % 4], 16)

        @block.scalar
        def _(act):
            s = nc.scalar
            for g in range(4):
                act.wait_ge(s_tr, g + 1)
                s.copy(xnT[:, 512 * g:512 * (g + 1)], P8[g][:, :]).then_inc(s_xnT, 1)
            act.wait_ge(s_dn, 1)
            s.activation(fd[:, :, :, HD], dnD[:, :, :], ACT.Exp).then_inc(s_exp, 1)
            act.wait_ge(s_dn, 2)
            s.activation(fb[:, :, :, HD], dnB[:, :, :], ACT.Exp).then_inc(s_exp, 1)
            act.wait_ge(s_dn, 4)
            s.activation(eA[:], tmn[:], ACT.Exp).then_inc(s_exp, 1)
            s.activation(eC[:], tmn2[:], ACT.Exp).then_inc(s_exp, 1)
            for n in range(4 * H):
                h, c = divmod(n, 4)
                act.wait_ge(s_src, n + 1)
                s.copy(srcb[:, h, c // 2, 512 * (c % 2):512 * (c % 2) + 512], P8[n % 4][:, :]).then_inc(s_srcs, 1)

            with act.Fori(0, T // 2) as k:
                for r in range(2):
                    act.wait_ge(s_mtr, k * 2 + (r + 1))
                    s.copy(maskT[:, :, bass.ds(k * (2 * P) + P * r, P)],
                           banks[:, 2 * r:2 * r + 2, :].rearrange("p b n -> p (b n)").bitcast(BF16)
                           .rearrange("p (j i) -> p j i", j=T)).then_inc(s_mT, 1)


            def steps(h, first):
                for j, n in enumerate(ON_ACT):
                    blk, jt = divmod(n, T)
                    if j >= RZ:
                        act.wait_ge(s_z, h * UNITS + (ON_ACT[j - RZ] + 1))
                    elif not first:
                        last = max(m for m in range(len(ON_ACT)) if m % RZ == j)
                        act.wait_ge(s_z, h * UNITS + (ON_ACT[last] + 1 - UNITS))
                    else:
                        act.wait_ge(s_fd, 1)
                    src_row = srcb[:, h, blk, :] if first else srcb[:, bass.ds(h, 1), blk, :].rearrange("p a n -> p (a n)")
                    bias = dsteep[:, h, jt:jt + 1] if first else dsteep[:, bass.ds(h, 1), jt]
                    if not first:
                        act.sem_inc(s_turn, 1)
                    s.activation(step_t[j % RZ], src_row, ACT.Sigmoid, bias=bias, scale=STEEP).then_inc(s_step, 1)

            act.wait_ge(s_srcs, 4 * H)
            steps(0, True)
            with act.Fori(1, H) as h:
                steps(h, False)

            for g in range(4):
                act.wait_ge(s_tr, 4 + g + 1)
                s.copy(xn2T[:, 512 * g:512 * (g + 1)], P8[g][:, :]).then_inc(s_xnT, 1)
            s.copy(row_k[1][:, :, 0:D], xn2).then_inc(s_rowB, 1)
            act.wait_ge(s_m2, 1)
            s.activation(e2[:], e2[:], ACT.Exp).then_inc(s_w2e, 1)

            def expert_step(tile):
                p = tile + -1
                if p.within(Q):
                    act.wait_ge(s_hp, p.count(1))
                    wait_from_first(act, s_hid, p.count(-1))
                    s.activation(silu_t[p.c % 2], P8[2 + p.c % 2][:, 0:F], ACT.Silu).then_inc(s_si, 1)
                p = tile + -2
                if p.within(Q):
                    act.wait_ge(s_t2, p.count(1))
                    wait_from_first(act, s_y, p.count(-1))
                    s.copy(hidT_t[p.c % 2], P8[4 + p.c % 2][:, 0:F]).then_inc(s_hT, 1)
            over_tiles(act, expert_step)

        @block.vector
        def _(dve):
            v = nc.vector
            chain = Chain(dve, s_dve)
            run, post = chain.run, chain.post

            def norm_stats(rows_in):
                for t in range(T):
                    post(v.bn_stats(stat[:, t, :], rows_in[:, t, :]))
                chain.wait()
                post(v.tensor_tensor(mean[:], stat[:, :, 1], stat[:, :, 4], ALU.add))
                post(v.tensor_tensor(st1[:], stat[:, :, 1], stat[:, :, 4], ALU.subtract))
                post(v.tensor_tensor(st2[:], stat[:, :, 2], stat[:, :, 5], ALU.add))
                chain.wait()
                post(v.tensor_scalar(mean[:], mean[:], 0.5, None, ALU.mult))
                post(v.tensor_tensor(st1[:], st1[:], st1[:], ALU.mult))
                post(v.tensor_scalar(st2[:], st2[:], 1.0 / D, EPS, ALU.mult, ALU.add))
                chain.wait()
                v.scalar_tensor_tensor(vare[:], st1[:], 0.25, st2[:], ALU.mult, ALU.add).then_inc(s_var, 1)

            def normalise(rows_out, rows_in, k):
                dve.wait_ge(s_rstd, k)
                for t in range(T):
                    post(v.tensor_scalar(rows_out[:, t, :], rows_in[:, t, :], mean[:, t:t + 1], rstd[:, t:t + 1],
                                         ALU.subtract, ALU.mult))
                chain.wait()

            dve.wait_ge(s_xld, 16)
            norm_stats(x_sb)
            dve.wait_ge(s_rstd, 1)
            for t in range(T):
                v.tensor_scalar(xn[:, t, :], x_sb[:, t, :], mean[:, t:t + 1], rstd[:, t:t + 1],
                                ALU.subtract, ALU.mult).then_inc(s_xn, 1)
            dve.wait_ge(s_wT, 1)
            v.tensor_copy(wT, P8[4][:, 0:P]).then_inc(s_wTs, 1)
            dve.wait_ge(s_wa, 1)
            run(v.tensor_copy(w_ext[:, D:HW], P8[5][:, 0:2 * H]))
            for h in range(H):
                v.tensor_scalar(w_src[:, h, :], ones_f, w_ext[:, D + h:D + h + 1], None, ALU.mult).then_inc(s_wext, 1)
            for g in range(6):
                n = min(3, T - 3 * g)
                dve.wait_ge(s_h, g + 1)
                v.tensor_copy(hh[:, 3 * g:3 * g + n, :],
                              P8[6 + g % 2][:, 0:n * HW].rearrange("p (t c) -> p t c", t=n)).then_inc(s_hs, 1)
            dve.wait_ge(s_hs, 6)
            src, dst = hh[:, :, D:D + H], hh[:, :, D + H:HW]
            v.tensor_reduce(dloc[:], dst.rearrange("p t h -> p h t"), AX.X, ALU.max).then_inc(s_dloc, 1)
            post(v.tensor_scalar(ndst[:].rearrange("p h t -> p t h"), dst, -1.0, None, ALU.mult))
            post(v.tensor_scalar(dsteep[:].rearrange("p h t -> p t h"), dst, STEEP, None, ALU.mult))
            dve.wait_ge(s_dmax, 1)
            dmax_b = dmax[:, :].unsqueeze(1).to_broadcast([P, T, H])
            post(v.tensor_tensor(dn[:], dst, dmax_b, ALU.subtract))
            post(v.tensor_tensor(tt[:], src, dmax_b, ALU.add))
            chain.wait()
            v.tensor_scalar(dnD[:], dn[:], 0.2, SHIFT, ALU.mult, ALU.add).then_inc(s_dn, 1)
            v.tensor_scalar(dnB[:], dn[:], SHIFT, None, ALU.add).then_inc(s_dn, 1)
            v.tensor_scalar(tmn[:], tt[:], 0.8, 0.0, ALU.mult, ALU.min).then_inc(s_dn, 1)
            v.tensor_scalar(tmn2[:], tt[:], -0.8, 0.0, ALU.mult, ALU.min).then_inc(s_dn, 1)
            dve.wait_ge(s_exp, 1)
            cut(v, chain, fd, hh, C1, s_fd)

            def mask(r):
                v.tensor_scalar(mask_t[r], adj_t[r], 0.0, None, ALU.is_gt).then_inc(s_mask, 1)

            def s0_sum(r, to):
                v.tensor_reduce(to, P8[4 + r][:, 0:3 * H * C1].rearrange("p (h k c) -> p h c k", h=H, k=3),
                                AX.X, ALU.add).then_inc(s_s0f, 1)

            for r in range(2):
                dve.wait_ge(s_adj[r], 16)
                mask(r)
            with dve.Fori(1, T // 2) as k:
                for r in range(2):
                    dve.wait_ge(s_adj[r], k * 16 + 16)
                    dve.wait_ge(s_mtr, k * 2 + (r - 1))
                    mask(r)
                    dve.wait_ge(s_s0, k * 2 + (r - 1))
                    s0_sum(r, S0[:, bass.ds(k * 2 + (r - 2), 1), :, :].rearrange("p a h c -> p (a h) c"))
            for r in range(2):
                dve.wait_ge(s_s0, T - 1 + r)
                s0_sum(r, S0[:, T - 2 + r, :, :])

            def z1(h, first):
                for n in range(UNITS):
                    blk, jt = divmod(n, T)
                    if not first or n >= RZ:
                        dve.wait_ge(s_zu, h * UNITS + (n + 1 - RZ))
                    z0 = maskT[:, jt, BW * blk:BW * (blk + 1)]
                    if n in ON_DVE:
                        src_row = srcb[:, h, blk, :] if first else \
                            srcb[:, bass.ds(h, 1), blk, :].rearrange("p a n -> p (a n)")
                        nd = ndst[:, h, jt:jt + 1] if first else ndst[:, bass.ds(h, 1), jt]
                        v.scalar_tensor_tensor(z_t[n % RZ], src_row, nd, z0, ALU.is_gt, ALU.mult).then_inc(s_z, 1)
                    else:
                        j = ON_ACT.index(n)
                        dve.wait_ge(s_step, h * len(ON_ACT) + (j + 1))
                        v.tensor_tensor(z_t[n % RZ], step_t[j % RZ], z0, ALU.mult).then_inc(s_z, 1)
                    if n == T + 2:
                        s1_sum(h, 0, h, first)
                    if n == 2 and not first:
                        s1_sum(h, 1, h - 1, False)

            def s1_sum(h, blk, hp, known):
                for b in range(4):
                    dve.wait_ge(s_zu, hp * UNITS + T * (blk + 1))
                    it = BT * blk + 2 * b
                    to = s1[:, hp, it:it + 2, :] if known else \
                        s1[:, bass.ds(hp, 1), it:it + 2, :].rearrange("p a i c -> p (a i) c")
                    v.tensor_reduce(to, P8[4 * blk + b][:, 0:6 * C2].rearrange("p (i k c) -> p i c k", i=2, k=3),
                                    AX.X, ALU.add).then_inc(s_acc, 1)

            dve.wait_ge(s_srcs, 4 * H)
            dve.wait_ge(s_mT, T)
            dve.wait_ge(s_fd, 1)
            dve.wait_ge(s_fb, 1)
            z1(0, True)
            with dve.Fori(1, H) as h:
                z1(h, False)
            s1_sum(H, 1, H - 1, True)
            dve.wait_ge(s_acc, 8 * H)
            dve.wait_ge(s_s0f, T)

            dve.wait_ge(s_exp, 4)
            s1B = s1[:, :, :, 0:C1].rearrange("p h t c -> p t h c")
            s1D = s1[:, :, :, C1:C2].rearrange("p h t c -> p t h c")
            post(v.tensor_tensor(S0[:], S0[:], s1D, ALU.subtract))
            post(v.tensor_tensor(s1B, s1B, eA[:].unsqueeze(3).to_broadcast([P, T, H, C1]), ALU.mult))
            chain.wait()
            run(v.tensor_tensor(S0[:], S0[:], eC[:].unsqueeze(3).to_broadcast([P, T, H, C1]), ALU.mult))
            run(v.tensor_tensor(S0[:], S0[:], s1B, ALU.add))
            run(v.reciprocal(rden[:], S0[:, :, :, HD]))
            run(v.tensor_tensor(gat.rearrange("p t (h c) -> p t h c", h=H), S0[:, :, :, 0:HD],
                                rden[:].unsqueeze(3).to_broadcast([P, T, H, HD]), ALU.mult))
            norm_stats(gat)
            normalise(tmp, gat, 2)
            dve.wait_ge(s_gld, 64)
            run(v.tensor_tensor(tmp, tmp, gam[:, :].unsqueeze(1).to_broadcast([P, T, D]), ALU.mult))
            run(v.tensor_tensor(tmp, tmp, bet[:, :].unsqueeze(1).to_broadcast([P, T, D]), ALU.add))
            dve.wait_ge(s_xld, 32)
            run(v.tensor_tensor(x1, tmp, x_again, ALU.add))
            norm_stats(x1)
            dve.wait_ge(s_rstd, 3)
            for t in range(T):
                v.tensor_scalar(xn2[:, t, :], x1[:, t, :], mean[:, t:t + 1], rstd[:, t:t + 1],
                                ALU.subtract, ALU.mult).then_inc(s_xn, 1)

            dve.wait_ge(s_lg, 1)
            run(v.tensor_tensor(lg, P8[4][:, 0:T * E].rearrange("p (t e) -> p t e", t=T),
                                gb[:, :].unsqueeze(1).to_broadcast([P, T, E]), ALU.add))

            def over_e(one_per_token):
                return one_per_token[:, :].unsqueeze(2).to_broadcast([P, T, E])
            order = first_e[:, :].unsqueeze(1).to_broadcast([P, T, E])

            def choose(logits, top, chosen):
                run(v.tensor_reduce(top[:], logits, AX.X, ALU.max))
                run(v.tensor_tensor(eq, logits, over_e(top), ALU.is_equal))
                run(v.tensor_tensor(eq, eq, order, ALU.mult))
                run(v.tensor_reduce(key1[:], eq, AX.X, ALU.max))
                run(v.tensor_tensor(chosen, order, over_e(key1), ALU.is_equal))
            choose(lg, m1, M1)
            run(v.scalar_tensor_tensor(lg2, M1, -BIG, lg, ALU.mult, ALU.add))
            choose(lg2, m2, M2)
            v.tensor_tensor(Mb[:], M1, M2, ALU.add).then_inc(s_M, 1)
            v.tensor_tensor(e2[:], m2[:], m1[:], ALU.subtract).then_inc(s_m2, 1)
            dve.wait_ge(s_rank, 1)
            run(v.tensor_tensor(eq, P8[5][:, 0:T * E].rearrange("p (t e) -> p t e", t=T),
                                region[:, :].unsqueeze(1).to_broadcast([P, T, E]), ALU.add))
            post(v.tensor_tensor(M1, M1, eq, ALU.mult))
            post(v.tensor_tensor(M2, M2, eq, ALU.mult))
            chain.wait()
            post(v.tensor_reduce(slot_f[:, 0, :], M1, AX.X, ALU.add))
            post(v.tensor_reduce(slot_f[:, 1, :], M2, AX.X, ALU.add))
            chain.wait()
            v.tensor_copy(slot_i[:], slot_f[:]).then_inc(s_slot, 1)
            dve.wait_ge(s_w2e, 1)
            run(v.tensor_scalar(wt2[:], e2[:], 1.0, None, ALU.add))
            run(v.reciprocal(wt1[:], wt2[:]))
            post(v.tensor_tensor(wt2[:], e2[:], wt1[:], ALU.mult))
            v.tensor_copy(row_k[0][:, :, D].bitcast(I32), goes_to[:, 0, :]).then_inc(s_rowA, 1)
            v.tensor_copy(row_k[0][:, :, D + 1], wt1[:]).then_inc(s_rowA, 1)
            chain.wait()
            v.tensor_copy(row_k[1][:, :, D].bitcast(I32), goes_to[:, 1, :]).then_inc(s_rowC, 1)
            v.tensor_copy(row_k[1][:, :, D + 1], wt2[:]).then_inc(s_rowC, 1)
            dve.wait_ge(s_rank, 2)
            run(v.tensor_copy(cnt[:], P8[6][:, 0:E]))
            run(v.tensor_tensor(pad_f[:], cnt[0:1, :], region[0:1, :], ALU.add))
            v.tensor_copy(pad_at[:], pad_f[:]).then_inc(s_pads, 1)
            run(v.tensor_tensor(big3, cnt[:, :].unsqueeze(2).to_broadcast([P, E, T]),
                                k128[:, :].unsqueeze(1).to_broadcast([P, E, T]), ALU.is_gt))
            run(v.tensor_reduce(ntile[:], big3, AX.X, ALU.add))
            run(v.tensor_tensor(tri, lt_e[:], ntile[:, :].unsqueeze(1).to_broadcast([P, E, E]), ALU.mult))
            run(v.tensor_reduce(base[:], tri, AX.X, ALU.add))
            post(v.tensor_tensor(endq[:], base[:], ntile[:], ALU.add))
            post(v.scalar_tensor_tensor(off_e[:], base[0:1, :], -float(P), region[0:1, :], ALU.mult, ALU.add))
            chain.wait()
            run(v.tensor_tensor(cmpq, endq[0:1, :].unsqueeze(1).to_broadcast([1, Q, E]),
                                qtile[0:1, :].unsqueeze(2).to_broadcast([1, Q, E]), ALU.is_le))
            run(v.tensor_reduce(eid_f[:], cmpq, AX.X, ALU.add))
            run(v.tensor_tensor(hotq, e_row[0:1, :].unsqueeze(1).to_broadcast([1, Q, E]),
                                eid_f[0:1, :].unsqueeze(2).to_broadcast([1, Q, E]), ALU.is_equal))
            run(v.tensor_tensor(hotq, hotq, off_e[0:1, :].unsqueeze(1).to_broadcast([1, Q, E]), ALU.mult))
            post(v.tensor_reduce(at_f[:], hotq, AX.X, ALU.add))
            run(v.tensor_scalar(live[:], eid_f[:], float(E), None, ALU.is_lt))
            post(v.scalar_tensor_tensor(at_f[:], qtile[:], float(P), at_f[:], ALU.mult, ALU.add))
            post(v.tensor_scalar(eid_f[:], eid_f[:], float(E - 1), None, ALU.min))
            chain.wait()
            run(v.tensor_scalar(at_f[:], at_f[:], pad_f[0:1, 0:1], None, ALU.subtract))
            run(v.tensor_tensor(at_f[:], at_f[:], live[:], ALU.mult))
            run(v.tensor_scalar(at_f[:], at_f[:], pad_f[0:1, 0:1], None, ALU.add))
            run(v.tensor_copy(place[:], at_f[:]))
            v.tensor_copy(eid[:, 4:4 + Q], eid_f[:]).then_inc(s_eid, 1)

            def expert_step(tile):
                if tile.within(Q):
                    dve.wait_ge(s_t1, tile.count(1))
                    wait_from_first(dve, s_hp, tile.count(-3))
                    v.tensor_copy(xgT_t[tile.c % 4], P8[tile.c % 2][:, 0:P]).then_inc(s_xgT, 1)
                p = tile + -1
                if p.within(Q):
                    dve.wait_ge(s_si, p.count(1))
                    wait_from_first(dve, s_t2, p.count(-1))
                    v.tensor_tensor(hid_t[p.c % 2], silu_t[p.c % 2], P8[2 + p.c % 2][:, F:2 * F],
                                    ALU.mult).then_inc(s_hid, 1)
                p = tile + -3
                if p.within(Q):
                    dve.wait_ge(s_y, p.count(1))
                    wait_from_first(dve, s_yst[p.c % 4], p.round(4) * 16)
                    v.tensor_scalar(y_t[p.c % 4], P8[6 + p.c % 2][:, 0:D], xg_t[p.c % RING][:, D + 1:D + 2], None,
                                    ALU.mult).then_inc(s_ys, 1)
            over_tiles(dve, expert_step)

            n = T // 4
            for g in range(4):
                part = slice(n * g, n * (g + 1))
                dve.wait_ge(s_gath[g], 16)
                run(v.tensor_tensor(tmp[:, part, :], y_pair[:, part, 0:D], y_pair[:, part, D:2 * D], ALU.add))
                v.tensor_tensor(tmp[:, part, :], tmp[:, part, :], x1[:, part, :], ALU.add).then_inc(s_fin, 1)

        @block.tensor
        def _(pe):
            mm, tp = nc.tensor.matmul, nc.tensor.transpose
            pe.wait_ge(s_wld, 16)
            pe.wait_ge(s_const, 1)
            tp(P8[4][:, 0:P], w_ext[:, 0:D], ident[:]).then_inc(s_wT, 1)
            pe.wait_ge(s_wTs, 1)
            pe.wait_ge(s_ald, 16 * 2 * H)
            mm(P8[5][:, 0:2 * H], wT, a_blk[:], start=True, stop=True).then_inc(s_wa, 1)
            for g in range(4):
                pe.wait_ge(s_xn, 4 * (g + 1))
                for t in range(4):
                    last = tp(P8[g][:, P * t:P * (t + 1)], xn[:, 4 * g + t, :], ident[:])
                last.then_inc(s_tr, 1)
            pe.wait_ge(s_xnT, 4)
            pe.wait_ge(s_wext, H)
            for g in range(6):
                if g >= 2:
                    pe.wait_ge(s_hs, g - 1)
                for t in range(3 * g, min(3 * g + 3, T)):
                    last = mm(P8[6 + g % 2][:, HW * (t - 3 * g):HW * (t - 3 * g + 1)], xnT[:, P * t:P * (t + 1)],
                              w_ext[:, :], start=True, stop=True)
                last.then_inc(s_h, 1)
            for n in range(4 * H):
                h, c = divmod(n, 4)
                if n >= 4:
                    pe.wait_ge(s_srcs, n - 3)
                mm(P8[n % 4][:, :], w_src[:, h, :], xnT[:, 512 * c:512 * (c + 1)], start=True, stop=True
                   ).then_inc(s_src, 1)
            pe.wait_ge(s_srcs, 4 * H)

            def transpose_mask(r):
                for j in range(T):
                    last = tp(P8[2 * r + j // 8][:, 64 * (j % 8):64 * (j % 8 + 1)].bitcast(BF16),
                              mask_t[r][:, P * j:P * (j + 1)], ident_b[:])
                last.then_inc(s_mtr, 1)

            def s0_products(r, rows_of):
                for j in range(T):
                    last = mm(P8[4 + r][:, 0:3 * H * C1], maskT[:, j, rows_of],
                              feat[:, :, j, :, C1:C2], start=(j == 0), stop=(j == T - 1))
                last.then_inc(s_s0, 1)

            for r in range(2):
                pe.wait_ge(s_mask, r + 1)
                transpose_mask(r)
                if r == 1:
                    pe.wait_ge(s_mT, 1)
                    pe.wait_ge(s_fd, 1)
                    s0_products(0, slice(0, P))
            with pe.Fori(1, T // 2) as k:
                for r in range(2):
                    pe.wait_ge(s_mask, k * 2 + (r + 1))
                    pe.wait_ge(s_mT, k * 2 + (r - 1))
                    transpose_mask(r)
                    pe.wait_ge(s_mT, k * 2 + r)
                    pe.wait_ge(s_s0f, k * 2 + (r - 2))
                    if r == 1:
                        s0_products(0, bass.ds(k * (2 * P), P))
                    else:
                        s0_products(1, bass.ds(k * (2 * P) - P, P))
            pe.wait_ge(s_mT, T)
            pe.wait_ge(s_s0f, T - 2)
            s0_products(1, slice(P * (T - 1), P * T))

            def z1_products(h, first):
                for n in range(UNITS):
                    blk, jt = divmod(n, T)
                    pe.wait_ge(s_z, h * UNITS + (n + 1))
                    moving = feat[:, h, jt, :, :].rearrange("p k c -> p (k c)") if first else \
                        feat[:, bass.ds(h, 1), jt, :, :].rearrange("p a k c -> p (a k c)")
                    for i in range(BT):
                        b = 4 * blk + i // 2
                        if jt == 0 and i % 2 == 0 and not first:
                            pe.wait_ge(s_acc, h * 8 + (b + 1 - 8))
                        last = mm(P8[b][:, 3 * C2 * (i % 2):3 * C2 * (i % 2 + 1)], z_t[n % RZ][:, P * i:P * (i + 1)],
                                  moving, start=(jt == 0 and i % 2 == 0), stop=(jt == T - 1), skip_group_check=True)
                    last.then_inc(s_zu, 1)
            pe.wait_ge(s_s0f, T)
            pe.wait_ge(s_fb, 1)
            z1_products(0, True)
            with pe.Fori(1, H) as h:
                z1_products(h, False)

            pe.wait_ge(s_acc, 8 * H)
            for g in range(4):
                pe.wait_ge(s_xn, T + 4 * (g + 1))
                for t in range(4):
                    last = tp(P8[g][:, P * t:P * (t + 1)], xn2[:, 4 * g + t, :], ident[:])
                last.then_inc(s_tr, 1)
            pe.wait_ge(s_xnT, 8)
            pe.wait_ge(s_gld, 64)
            for t in range(T):
                last = mm(P8[4][:, E * t:E * (t + 1)], xn2T[:, P * t:P * (t + 1)], gw[:], start=True, stop=True)
            last.then_inc(s_lg, 1)
            pe.wait_ge(s_M, 1)
            mm(P8[5][:, 0:T * E], before[:], Mb[:, :, :].rearrange("p t e -> p (t e)"), start=True, stop=False)
            for t in range(T - 1):
                last = mm(P8[5][:, E * (t + 1):T * E].rearrange("p (t e) -> p t e", e=E), ones_b[:],
                          Mb[:, t:t + 1, :].to_broadcast([P, T - 1 - t, E]), start=False, stop=(t == T - 2))
            last.then_inc(s_rank, 1)
            for t in range(T):
                last = mm(P8[6][:, 0:E], ones_b[:], Mb[:, t, :], start=(t == 0), stop=(t == T - 1))
            last.then_inc(s_rank, 1)

            pe.wait_ge(s_w12, 32)
            pe.wait_ge(s_w3, 16)
            pe.wait_ge(s_eid, 1)

            experts = [pe.alloc_register(f"expert{n}") for n in range(8)]

            def load_experts(tile):
                at = slice(tile.count(), tile.count(8)) if tile.known() else bass.ds(tile.count(), 8)
                pe.load(experts, eid[0:1, at])

            def expert_of(n):
                return pe.snap(experts[n], min_val=0, max_val=E - 1)

            load_experts(Tile(0, 0))

            def expert_step(tile):
                if tile.within(Q):
                    r = tile.c % RING
                    pe.wait_ge(s_xg[r], tile.round(RING, 1) * 16)
                    wait_from_first(pe, s_xgT, tile.count(-1))
                    tp(P8[tile.c % 2][:, 0:P], xg_t[r][:, 0:D], ident[:]).then_inc(s_t1, 1)
                p = tile + -1
                if p.within(Q):
                    e = expert_of(3 + tile.c % 4)
                    pe.wait_ge(s_xgT, p.count(1))
                    wait_from_first(pe, s_hid, p.count(-1))
                    mm(P8[2 + p.c % 2][:, :], xgT_t[p.c % 4], R1[:, bass.ds(e * (2 * F), 2 * F)],
                       start=True, stop=True).then_inc(s_hp, 1)
                if (tile + -3).within(Q):
                    e = expert_of(1 + tile.c % 4)
                if tile.c % 4 == 3:
                    load_experts(tile + 1)
                p = tile + -2
                if p.within(Q):
                    pe.wait_ge(s_hid, p.count(1))
                    wait_from_first(pe, s_hT, p.count(-1))
                    for c in range(FC):
                        last = tp(P8[4 + p.c % 2][:, P * c:P * (c + 1)], hid_t[p.c % 2][:, P * c:P * (c + 1)], ident[:])
                    last.then_inc(s_t2, 1)
                p = tile + -3
                if p.within(Q):
                    pe.wait_ge(s_hT, p.count(1))
                    wait_from_first(pe, s_ys, p.count(-1))
                    for c in range(FC):
                        last = mm(P8[6 + p.c % 2][:, 0:D], hidT_t[p.c % 2][:, P * c:P * (c + 1)],
                                  late[:, bass.ds(e * (FC * D) + c * D, D)], start=(c == 0), stop=(c == FC - 1))
                    last.then_inc(s_y, 1)
            over_tiles(pe, expert_step)


_INS = ["x", "adj", "L0_gnn_W", "L0_gnn_a", "L0_gnn_gamma", "L0_gnn_beta", "L0_ffn_gate_w", "L0_ffn_gate_b",
        "L0_ffn_w1", "L0_ffn_w2", "L0_ffn_w3"]


def kernel(**inputs):
    import numpy as np
    import concourse.bacc as bacc
    from concourse.bass_utils import run_bass_kernel_spmd

    nc = bacc.Bacc("TRN2", target_bir_lowering=False, num_devices=1)
    arrays, args = {}, []
    for name in _INS:
        array = np.ascontiguousarray(inputs[name])
        arrays[name] = array
        args.append(nc.dram_tensor(name, array.shape, F32, kind="ExternalInput").ap())
    out = nc.dram_tensor("out", inputs["x"].shape, F32, kind="ExternalOutput").ap()
    build(nc, *args, out)
    got = run_bass_kernel_spmd(nc, [arrays], core_ids=[0])
    return got.results[0]["out"]
```

```python
from contextlib import ExitStack

import concourse.bass as bass
from concourse import mybir

F32 = mybir.dt.float32
BF16 = mybir.dt.bfloat16
I32 = mybir.dt.int32
ALU = mybir.AluOpType
ACT = mybir.ActivationFunctionType
AX = mybir.AxisListType

P = 128
EPS = 1e-5
SHIFT = 60.0
STEEP = 1e20
BIG = 3.0e38


class Chain:

    def __init__(self, engine, sem):
        self.engine, self.sem, self.n = engine, sem, 0

    def post(self, instruction):
        self.n += 1
        instruction.then_inc(self.sem, 1)

    def wait(self):
        self.engine.wait_ge(self.sem, self.n)

    def run(self, instruction):
        self.post(instruction)
        self.wait()


RING = 8


class Tile:

    def __init__(self, k, c):
        self.k, self.c = k, c

    def __add__(self, n):
        return Tile(self.k, self.c + n)

    def count(self, n=0):
        return self.k * RING + (self.c + n)

    def round(self, size, n=0):
        return self.k * (RING // size) + (self.c // size + n)

    def known(self):
        return isinstance(self.k, int)

    def within(self, total):
        return not self.known() or 0 <= self.count() < total


def wait_from_first(engine, sem, value):
    if not isinstance(value, int) or value > 0:
        engine.wait_ge(sem, value)


def build(nc, x, adj, w, a, gamma, beta, gate_w, gate_b, w1, w2, w3, out):
    N, D = x.shape
    T = N // P
    HD = a.shape[0] // 2
    H = w.shape[1] // HD
    E, _, F = w1.shape
    C1 = HD + 1
    C2 = 2 * C1
    BLK = 2
    BT = T // BLK
    BW = BT * P
    TILES = 2 * T + E - 1
    Q = -(-TILES // RING) * RING
    REGION = N + P
    ROW = D + 2
    ADJ = 5
    ADJ_PLACE = [0, 2, 1, 3, 4, 0, 2, 1]
    RS, RZ = 6, 8
    ON_DVE = [0, 3, 11, 12]
    ON_DVE_2 = [[], [], [2, 7], []]
    ON_ACT = [n for n in range(T) if n not in ON_DVE]
    STEPS = [h * T + n for h in range(H) for n in ON_ACT]
    STEPS += [(H + h) * T + n for h in range(H) for n in range(T) if n not in ON_DVE_2[h]]
    FC = F // P
    G = 8
    S0_BEFORE = {0: 8, 16: 10, 32: 12, 49: 15}
    S0_FROM = {2: 9, 16: 11, 33: 13, 40: 14}
    S0_AT = [4, 13, 22, 29, 36, 46, 51, 55]
    DIV_AT, STATS_AT = 21, 36
    CHOOSE_AT, SLOTS_AT = 44, 61
    TR_AT, LOGITS_AT, RANKS_AT = 33, 39, 54
    X1T_AT, ROWS2_AT, WEIGHTS_AT = [41, 42], 46, 53
    DIV2_AT = 63

    xg = nc.dram_tensor("slots", (E * REGION, ROW), F32, kind="Internal").ap()
    src_dram = nc.dram_tensor("src_rows", (H, N), F32, kind="Internal").ap()
    yg = nc.dram_tensor("expert_rows", (2 * N, D), F32, kind="Internal").ap()
    yg_v = yg.rearrange("(t p k) d -> p t (k d)", k=2, p=P)
    x_v = x.rearrange("(t p) d -> p t d", p=P)
    out_v = out.rearrange("(t p) d -> p t d", p=P)

    ctx = ExitStack()
    with ctx:
        def sb(name, shape, dt=F32):
            return ctx.enter_context(nc.sbuf_tensor(name, shape, dt))

        def sem(name):
            return ctx.enter_context(nc.semaphore(name))

        R1 = sb("R1", [P, 8192])
        srcb = sb("srcb", [P, H, BLK, BW])
        maskT = sb("maskT", [P, BLK, T, BW], BF16)
        feat = sb("feat", [P, H, T, 3, C2], BF16)
        ring = sb("ring", [P, 512 * (RS + 4)])
        S0 = sb("S0", [P, T, H, C1])
        HW = D + 2 * H
        S1 = sb("S1", [P, BT * H * C2 + T * HW])

        def adj_slot(tile):
            return ADJ_PLACE[tile] if tile < BT else (2 if tile % 2 == 0 else 0)

        def tile_before(tile):
            return max((t for t in range(tile) if adj_slot(t) == adj_slot(tile)), default=None)
        adj_t = [R1[:, 0:N], R1[:, N:2 * N], R1[:, 6144:6144 + N]]
        adj_t += [srcb[:, h, :, :].rearrange("p b n -> p (b n)") for h in range(H - 2, H)]
        mask_t = [R1[:, 4096 + 1024 * r:5120 + 1024 * r].bitcast(BF16) for r in range(2)]
        w12 = R1[:, :].rearrange("p (e f) -> p e f", e=E)
        step_t = [ring[:, 512 * r:512 * (r + 1)].bitcast(BF16) for r in range(RS)]
        z_t = [place[:, first + 512 * r:first + 512 * (r + 1)].bitcast(BF16)
               for place, first in ((ring, 512 * RS), (R1, N)) for r in range(4)]
        x_sb = S1[:, 0:T * D].rearrange("p (t d) -> p t d", t=T)
        hh = S1[:, BT * H * C2:BT * H * C2 + T * HW].rearrange("p (t c) -> p t c", t=T)
        s0_flat = S0[:, :, :, :].rearrange("p t h c -> p (t h c)")
        f_pair = [place[:, 0:2 * T * C2].rearrange("p (h t b c) -> p h t b c", h=2, t=T, b=2)
                  for place in (S1, s0_flat)]
        s1 = [S1[:, BT * H * C2 * b:BT * H * C2 * (b + 1)].rearrange("p (h t c) -> p h t c", h=H, t=BT)
              for b in range(BLK)]

        half = [maskT[:, b, :, :].rearrange("p t n -> p (t n)").bitcast(F32) for b in range(BLK)]
        xn = half[1][:, 0:T * D].rearrange("p (t d) -> p t d", t=T)
        xnT = half[1][:, 2048:4096]
        src_rows = half[1][0:H, 6144:6144 + N]
        wT = half[1][:, 4096 + H * P:4096 + (H + 1) * P]
        dn, dnB, dnD, tt, tmn, tmn2 = [half[1][:, 5120 + T * H * k:5120 + T * H * (k + 1)]
                                       .rearrange("p (t h) -> p t h", t=T) for k in range(6)]
        w3_all = half[1][:, 0:4096]
        w3_sb = w3_all.rearrange("p (e c o) -> p e c o", e=E, c=FC)
        x_again = half[0][:, 0:2048].rearrange("p (t d) -> p t d", t=T)
        x1 = half[0][:, 2048:4096].rearrange("p (t d) -> p t d", t=T)
        tmp = half[0][:, 4096:6144].rearrange("p (t d) -> p t d", t=T)
        gat, normed = tmp[:, 0:BT, :], tmp[:, BT:T, :]
        x1T = half[0][:, 6144:6144 + BW]
        row_k = [[S1[:, 2112 * b + BT * ROW * k:2112 * b + BT * ROW * (k + 1)].rearrange("p (t c) -> p t c", t=BT)
                  for k in range(2)] for b in range(BLK)]
        flat = srcb[:, :, :, :].rearrange("p h b n -> p (h b n)")
        xgT_t = [flat[:, P * r:P * (r + 1)] for r in range(4)]
        y_t = [flat[:, 512 + P * r:512 + P * (r + 1)] for r in range(4)]
        silu_t = [flat[:, 1024 + F * r:1024 + F * (r + 1)] for r in range(2)]
        hid_t = [flat[:, 1536 + F * r:1536 + F * (r + 1)] for r in range(2)]
        hidT_t = [flat[:, 2048 + F * r:2048 + F * (r + 1)] for r in range(2)]
        xg_t = [flat[:, 2560 + ROW * r:2560 + ROW * (r + 1)] for r in range(RING)]
        y_pair = flat[:, 4096:8192].rearrange("p (t c) -> p t c", t=T)

        w_ext = sb("w_ext", [P, HW])
        a_blk = sb("a_blk", [P, 2 * H])
        ident = sb("ident", [P, P])
        ident_b = sb("ident_b", [P, P], BF16)
        gam = sb("gam", [P, D])
        bet = sb("bet", [P, D])
        gw = sb("gw", [P, E])
        gb = sb("gb", [P, E])
        stat = sb("stat", [P, T, 6])
        st1 = sb("st1", [P, T])
        st2 = sb("st2", [P, T])
        mean = sb("mean", [P, T])
        vare = sb("vare", [P, T])
        warm = sb("warm", [P, 1])
        rstd = sb("rstd", [P, T])
        neg_half = sb("neg_half", [P, T])
        dloc = sb("dloc", [P, H])
        dmax = sb("dmax", [P, H])
        ndst = sb("ndst", [P, H, T])
        dsteep = sb("dsteep", [P, H, T])
        eA = sb("eA", [P, T, H])
        eC = sb("eC", [P, T, H])
        rden = sb("rden", [P, T, H])
        pad_rows = sb("pad_rows", [P, ROW])
        before = sb("before", [P, P], BF16)
        ones_b = sb("ones_b", [P, P], BF16)
        first_e = sb("first_e", [P, E])
        lt_e = sb("lt_e", [P, E, E])
        k128 = sb("k128", [P, T])
        qtile = sb("qtile", [1, Q])
        region = sb("region", [P, E])
        e_row = sb("e_row", [1, E])
        goes_to = sb("goes_to", [P, 2, T], I32)

        banks = ctx.enter_context(nc.psum_tensor("banks", [P, 8, 512], F32))
        P8 = [banks[:, k, :] for k in range(8)]

        s_xld, s_xag = [sem(f"x_loaded{k}") for k in range(2)], sem("x_loaded_again")
        s_wld, s_ald, s_gld = sem("w_loaded"), sem("a_loaded"), sem("gb_loaded")
        s_ablk = sem("a_blk_zeroed")
        s_adj = [sem(f"adj_loaded{r}") for r in range(ADJ)]
        s_const = sem("constants_built")
        s_pool = sem("pool_steps")
        s_dve = sem("dve_steps")
        s_var = sem("variance_ready")
        s_warm = sem("sigmoid_table_loaded")
        s_rstd = sem("rstd_ready")
        s_xn = sem("xn_ready")
        s_tr = sem("transposes_done")
        s_xnT = sem("xnT_ready")
        s_wT = sem("wT_psum")
        s_wTs = sem("wT_sbuf")
        s_wa = sem("wa_psum")
        s_wext = sem("w_ext_ready")
        s_h = sem("h_psum")
        s_hs = sem("h_sbuf")
        s_src = sem("src_psum")
        s_srcs = sem("src_rows_copied")
        s_srco = sem("src_rows_stored")
        s_srcl = [sem(f"src_loaded{h}") for h in range(H)]
        s_dloc = sem("dloc_ready")
        s_dmax = sem("dmax_ready")
        s_dn = sem("exp_inputs_ready")
        s_exp = sem("exps_ready")
        s_f = sem("features_ready")
        s_part = sem("feature_parts_copied")
        s_cut = sem("first_heads_cut")
        s_cut2 = sem("last_heads_cut")
        s_num = sem("numerators_ready")
        s_shift = sem("shift_ready")
        s_xb = sem("beta_added")
        s_gcs = sem("gate_columns_summed")
        s_x1 = sem("x1_ready")
        s_mask = sem("mask_made")
        s_mtr = sem("mask_transposed")
        s_mT = sem("maskT_written")
        s_s0 = sem("s0_psum")
        s_s0f = sem("s0_evacuated")
        s_step = sem("step_made")
        s_turn = sem("step_turns")
        s_z = sem("z1_made")
        s_zu = sem("z1_used")
        s_acc = sem("acc_evacuated")
        s_w12 = sem("w12_loaded")
        s_w3 = sem("w3_loaded")
        s_pad = sem("slots_padded")
        s_pads = sem("pad_places_ready")
        s_rowA = sem("first_rows_columns")
        s_rowB = sem("second_rows_copied")
        s_rowC = sem("second_rows_columns")
        s_lg = sem("logits_psum")
        s_M = sem("choices_made")
        s_rank = sem("ranks_psum")
        s_slot = sem("slots_ready")
        s_wt = sem("weights_ready")
        s_dm = sem("logit_gap_ready")
        s_sc = sem("rows_scattered")
        s_xg = [sem(f"slot_tile_loaded{r}") for r in range(RING)]
        s_turn2 = sem("scatter_turns")
        s_t1 = sem("xg_transposed")
        s_xgT = sem("xgT_sbuf")
        s_hp = sem("hidden_psum")
        s_si = sem("silu_ready")
        s_hid = sem("hidden_ready")
        s_t2 = sem("hidden_transposed")
        s_hT = sem("hiddenT_sbuf")
        s_y = sem("y_psum")
        s_ys = sem("y_sbuf")
        s_yst = [sem(f"y_stored{r}") for r in range(4)]
        s_gath = [sem(f"y_gathered{g}") for g in range(G)]
        s_eid = sem("tile_experts_ready")
        s_fin = sem("out_ready")
        s_out = sem("out_stored")

        lg, lg2, eq, M1, M2 = [half[0][:, 7168 + P * k:7168 + P * (k + 1)].rearrange("p (t e) -> p t e", t=BT)
                               for k in range(5)]
        big3 = flat[:, 4096:4352].rearrange("p (e k) -> p e k", e=E)
        tri = flat[:, 4352:4608].rearrange("p (e f) -> p e f", e=E)
        cmpq = flat[0:1, 4608:4608 + Q * E].rearrange("p (q e) -> p q e", q=Q)
        hotq = flat[0:1, 5632:5632 + Q * E].rearrange("p (q e) -> p q e", q=Q)
        m1 = sb("m1", [P, BT])
        m2 = sb("m2", [P, BT])
        key1 = sb("key1", [P, BT])
        Mb = sb("Mb", [P, T, E], BF16)
        gcs = sb("gcs", [P, E])
        shift = sb("shift", [P, BT])
        gap = sb("gap", [P, BT])
        cnt = sb("cnt", [P, E])
        ntile = sb("ntile", [P, E])
        base = sb("base", [P, E])
        endq = sb("endq", [P, E])
        slot_f = sb("slot_f", [P, 2, BT])
        slot_i = sb("slot_i", [P, BLK, 2, BT], I32)
        eid_f = sb("eid_f", [1, Q])
        eid = sb("eid", [1, 4 + Q + 4], I32)
        at_f = sb("at_f", [1, Q])
        live = sb("live", [1, Q])
        place = sb("place", [1, Q], I32)
        off_e = sb("off_e", [1, E])
        pad_f = sb("pad_f", [1, E])
        pad_at = sb("pad_at", [1, E], I32)

        block = ctx.enter_context(nc.Block())

        PIECES = [(0, slice(0, 2)), (1, slice(1, 2)), (1, slice(0, 1))]

        def parts_of(h, bs=slice(0, 2)):
            columns = slice(C1 * bs.start, C1 * bs.stop)
            return [feat[:, h, :, k, columns] for k in range(3)], f_pair[h // 2][:, h % 2, :, bs, :]

        def times_columns(engine, h, bs=slice(0, 2)):
            _, f = parts_of(h, bs)
            wide = [P, T, bs.stop - bs.start, HD]
            return engine.tensor_tensor(f[:, :, :, 0:HD], hh[:, :, HD * h:HD * (h + 1)].unsqueeze(2).to_broadcast(wide),
                                        f[:, :, :, HD:C1].to_broadcast(wide), ALU.mult)

        def joined(f):
            return f.rearrange("p t b c -> p t (b c)")

        def sums_at(t):
            if isinstance(t, int):
                return S0[:, t, :, :]
            return S0[:, bass.ds(t, 1), :, :].rearrange("p a h c -> p (a h) c")

        def numerators(engine, chain, blk, heads):
            of = slice(BT * blk, BT * (blk + 1))
            sums = S0[:, of, heads, :]
            wide = [P, BT, heads.stop - heads.start, C1]
            s1B = s1[blk][:, heads, :, 0:C1].rearrange("p h t c -> p t h c")
            s1D = s1[blk][:, heads, :, C1:C2].rearrange("p h t c -> p t h c")
            chain.post(engine.tensor_tensor(sums, sums, s1D, ALU.subtract))
            chain.post(engine.tensor_tensor(s1B, s1B, eA[:, of, heads].unsqueeze(3).to_broadcast(wide), ALU.mult))
            chain.wait()
            chain.run(engine.tensor_tensor(sums, sums, eC[:, of, heads].unsqueeze(3).to_broadcast(wide), ALU.mult))
            engine.tensor_tensor(sums, sums, s1B, ALU.add).then_inc(s_num, 1)

        def load_a(engine, side):
            engine.wait_ge(s_ablk, 1)
            for h in range(H):
                engine.dma_start(a_blk[HD * h:HD * (h + 1), side * H + h:side * H + h + 1],
                                 a[HD * side:HD * (side + 1), :]).then_inc(s_ald, 16)

        def pad_experts(engine, half):
            engine.wait_ge(s_pads, 1)
            with engine.Fori(half * E // 2, (half + 1) * E // 2) as e:
                at = engine.value_load(pad_at[0:1, bass.ds(e, 1)], min_val=0, max_val=E * REGION - P)
                engine.dma_start(xg[bass.ds(at, P), :], pad_rows[:]).then_inc(s_pad, 16)

        def over_tiles(engine, step, after):
            for c in range(RING):
                step(Tile(0, c))
            with engine.Fori(1, TILES // RING) as k:
                for c in range(RING):
                    step(Tile(k, c))
            for c in range(TILES % RING + after):
                step(Tile(TILES // RING, c))

        @block.sync
        def _(sp):
            for half_of_x in range(2):
                of = slice(BT * half_of_x, BT * (half_of_x + 1))
                sp.dma_start(x_sb[:, of, :], x_v[:, of, :]).then_inc(s_xld[half_of_x], 16)
            sp.dma_start(w_ext[:, 0:D], w).then_inc(s_wld, 16)
            load_a(sp, 1)
            for tile in range(BT + 2):
                if tile == BT:
                    sp.wait_ge(s_srcs, 4)
                    sp.dma_start(src_dram, src_rows).then_inc(s_srco, 16)
                    sp.wait_ge(s_srco, 16)
                    for h in range(H):
                        if h == 2:
                            sp.wait_ge(s_mask, 5)
                        sp.dma_start(srcb[:, h, :, :].rearrange("p b n -> p (b n)"),
                                     src_dram[h:h + 1, :].rearrange("a n -> (a n)").partition_broadcast(P)
                                     ).then_inc(s_srcl[h], 16)
                if tile_before(tile) is not None:
                    sp.wait_ge(s_mask, tile_before(tile) + 1)
                sp.dma_start(adj_t[adj_slot(tile)], adj[P * tile:P * (tile + 1), :]).then_inc(s_adj[adj_slot(tile)], 16)
            with sp.Fori(1, BT // 2) as k:
                for r in range(2):
                    sp.wait_ge(s_mask, k * 2 + (BT + r - 1))
                    sp.dma_start(adj_t[adj_slot(BT + r)], adj[bass.ds(k * (2 * P) + P * (BT + r), P), :]
                                 ).then_inc(s_adj[adj_slot(BT + r)], 16)
            sp.wait_ge(s_z, T + H * T)
            sp.wait_ge(s_s0, BT)
            sp.dma_start(x_again, x_v).then_inc(s_xag, 16)
            sp.wait_ge(s_mtr, 2 * T)
            sp.wait_ge(s_zu, RZ + BLK * H * T)
            sp.dma_start(w12[:, :, 0:F], w1.rearrange("e d f -> d e f")).then_inc(s_w12, 16)
            sp.dma_start(w12[:, :, F:2 * F], w2.rearrange("e d f -> d e f")).then_inc(s_w12, 16)
            sp.wait_ge(s_z, T + BLK * H * T)
            sp.wait_ge(s_s0, T)
            sp.dma_start(w3_sb, w3.rearrange("e (c p) o -> p e c o", p=P)).then_inc(s_w3, 16)
            pad_experts(sp, 0)

            sp.wait_ge(s_eid, 1)
            sp.wait_ge(s_pad, 16 * E)
            sp.wait_ge(s_sc, 16 * 2 * T)

            def load_tile(tile):
                at = place[0:1, tile.count():tile.count(1)] if tile.known() else place[0:1, bass.ds(tile.count(), 1)]
                at = sp.value_load(at, min_val=0, max_val=E * REGION - P)
                if not tile.known() or tile.count() >= RING:
                    sp.wait_ge(s_yst[tile.c % 4], tile.round(4, 1 - RING // 4) * 16)
                sp.dma_start(xg_t[tile.c % RING], xg[bass.ds(at, P), :]).then_inc(s_xg[tile.c % RING], 16)
            over_tiles(sp, load_tile, 0)
            for r in range(4):
                sp.wait_ge(s_yst[r], 16 * len(range(r, TILES, 4)))
            for g in range(G):
                n = T // G
                sp.dma_start(y_pair[:, n * g:n * (g + 1), :], yg_v[:, n * g:n * (g + 1), :]).then_inc(s_gath[g], 16)
            for g in range(G):
                n = T // G
                sp.wait_ge(s_fin, g + 1)
                sp.dma_start(out_v[:, n * g:n * (g + 1), :], tmp[:, n * g:n * (g + 1), :]).then_inc(s_out, 16)
            sp.wait_ge(s_out, 16 * G)

        @block.gpsimd
        def _(pool):
            g = nc.gpsimd
            chain = Chain(pool, s_pool)
            g.memset(a_blk[:, :], 0.0).then_inc(s_ablk, 1)
            for tile, value in ((ident, 0.0), (neg_half, -0.5), (before, 1.0), (ones_b, 1.0),
                                (pad_rows, 0.0), (lt_e, 1.0)):
                chain.post(g.memset(tile[:, :], value))
            chain.wait()
            chain.run(g.affine_select(out=ident[:], in_=ident[:], compare_op=ALU.not_equal, fill=1.0, base=0,
                                      pattern=[[-1, P]], channel_multiplier=1))
            g.tensor_copy(ident_b[:], ident[:]).then_inc(s_const, 1)
            chain.post(g.affine_select(out=before[:], in_=before[:], compare_op=ALU.is_gt, fill=0.0, base=0,
                                       pattern=[[1, P]], channel_multiplier=-1))
            chain.post(g.affine_select(out=lt_e[:], in_=lt_e[:], compare_op=ALU.is_gt, fill=0.0, base=0,
                                       pattern=[[1, E], [-1, E]], channel_multiplier=0))
            for tile, step, count, first in ((first_e, -1, E, E), (k128, P, T, 0), (qtile, 1, Q, 0),
                                             (region, REGION, E, 0), (e_row, 1, E, 0)):
                chain.post(g.iota(tile[:], pattern=[[step, count]], base=first, channel_multiplier=0,
                                  allow_small_or_imprecise_dtypes=True))
            chain.post(g.iota(goes_to[:], pattern=[[1, 2], [2 * P, T]], base=0, channel_multiplier=2))
            chain.post(g.iota(pad_rows[:, D:D + 1].bitcast(I32), pattern=[[0, 1]], base=2 * N, channel_multiplier=0))
            chain.run(g.memset(eid[:], 0))

            def root(k, of):
                pool.wait_ge(s_var, k)
                g.tensor_tensor(rstd[:, of], vare[:, of], neg_half[:, of], ALU.pow).then_inc(s_rstd, 1)

            one_block = slice(0, BT)
            root(1, one_block)
            root(2, slice(BT, T))
            pool.wait_ge(s_dloc, 1)
            g.partition_all_reduce(dmax[:], dloc[:], P, bass.bass_isa.ReduceOp.max).then_inc(s_dmax, 1)
            pool.wait_ge(s_exp, 4)
            pool.wait_ge(s_hs, 6)
            for bs in (slice(1, 2), slice(0, 1)):
                for h in range(2, H):
                    part, f = parts_of(h, bs)
                    chain.run(times_columns(g, h, bs))
                    chain.run(g.tensor_copy(part[0], joined(f)))
                    chain.run(g.tensor_tensor(joined(f), joined(f), part[0], ALU.subtract))
                    chain.run(g.tensor_copy(part[1], joined(f)))
                    g.tensor_tensor(part[2], joined(f), part[1], ALU.subtract).then_inc(s_cut2, 1)

            def scatter(blk, k, tiles=range(BT)):
                pool.wait_ge(s_slot, 2 * blk + k + 1)
                if k == 0:
                    pool.wait_ge(s_xn, T + BT * (blk + 1))
                    pool.wait_ge(s_rowA, blk + 1)
                    pool.wait_ge(s_wt, 2 * blk + 1)
                else:
                    pool.wait_ge(s_rowB, blk + 1)
                    pool.wait_ge(s_rowC, blk + 1)
                    pool.wait_ge(s_wt, 2 * blk + 2)
                for t in tiles:
                    g.indirect_dma_start(
                        out=xg, out_offset=bass.IndirectOffsetOnAxis(ap=slot_i[:, blk, k, t:t + 1], axis=0),
                        in_=row_k[blk][k][:, t, :], in_offset=None).then_inc(s_sc, 16)

            pool.wait_ge(s_acc, 4 * H)
            pool.wait_ge(s_s0f, 2 + BT)
            pool.wait_ge(s_exp, 6)
            numerators(g, chain, 0, slice(0, H))
            pool.wait_ge(s_xag, 16)
            pool.wait_ge(s_gld, 64)
            g.tensor_tensor(x_again, x_again, bet[:, :].unsqueeze(1).to_broadcast([P, T, D]), ALU.add).then_inc(s_xb, 1)
            g.partition_all_reduce(gcs[:], gw[:], P, bass.bass_isa.ReduceOp.add).then_inc(s_gcs, 1)
            root(3, one_block)
            first, wide = slice(0, BT), [P, BT, D]
            mean_b, rstd_b = (part[:, first].unsqueeze(2).to_broadcast(wide) for part in (mean, rstd))
            chain.run(g.tensor_tensor(normed, gat, mean_b, ALU.subtract))
            chain.run(g.tensor_tensor(normed, normed, gam[:, :].unsqueeze(1).to_broadcast(wide), ALU.mult))
            pool.wait_ge(s_rstd, 3)
            chain.run(g.tensor_tensor(normed, normed, rstd_b, ALU.mult))
            pool.wait_ge(s_xb, 1)
            g.tensor_tensor(x1[:, first, :], normed, x_again[:, first, :], ALU.add).then_inc(s_x1, BT)
            root(4, one_block)
            pool.wait_ge(s_x1, BT)
            row = row_k[0][0][:, :, 0:D]
            chain.run(g.tensor_tensor(row, x1[:, first, :], mean_b, ALU.subtract))
            pool.wait_ge(s_rstd, 4)
            g.tensor_tensor(row, row, rstd_b, ALU.mult).then_inc(s_xn, BT)
            pool.wait_ge(s_acc, 4 * (2 * H - 1))
            pool.wait_ge(s_s0f, 2 + T)
            numerators(g, chain, 1, slice(0, H - 1))
            scatter(0, 0)
            root(5, one_block)
            scatter(0, 1, range(BT // 2))
            root(6, one_block)
            scatter(0, 1, range(BT // 2, BT))
            scatter(1, 0)
            scatter(1, 1)

            def scatter_results(tile):
                c = tile.c % RING
                pool.wait_ge(s_ys, tile.count(1))
                if not tile.known():
                    pool.sem_inc(s_turn2, 1)
                g.indirect_dma_start(
                    out=yg, out_offset=bass.IndirectOffsetOnAxis(ap=xg_t[c][:, D:D + 1].bitcast(I32), axis=0),
                    in_=y_t[c % 4], in_offset=None, bounds_check=2 * N - 1, oob_is_err=False,
                ).then_inc(s_yst[c % 4], 16)
            over_tiles(pool, scatter_results, 0)

        @block.scalar
        def _(act):
            s = nc.scalar
            load_a(act, 0)
            for dst, src in ((gam, gamma), (bet, beta), (gb, gate_b)):
                act.dma_start(dst[:], src.partition_broadcast(P)).then_inc(s_gld, 16)
            act.dma_start(gw[:], gate_w).then_inc(s_gld, 16)

            def write_maskT(tile):
                for b in range(2):
                    if isinstance(tile, int):
                        act.wait_ge(s_mtr, 2 * tile + b + 1)
                        to = maskT[:, tile // BT, 8 * b:8 * (b + 1), P * (tile % BT):P * (tile % BT + 1)]
                    else:
                        h, r = tile
                        act.wait_ge(s_mtr, h * 4 + (2 * (BT + r) + b + 1))
                        to = maskT[:, 1, 8 * b:8 * (b + 1), bass.ds(h * (2 * P) + P * r, P)]
                    s.copy(to, P8[6 + b].bitcast(BF16).rearrange("p (j i) -> p j i", i=P)).then_inc(s_mT, 1)

            def copy_part(i, k):
                part, f = parts_of(*PIECES[i])
                act.wait_ge(s_f, 2 * i + k + 1)
                s.copy(part[k], joined(f)).then_inc(s_part, 1)

            for g in range(4):
                act.wait_ge(s_tr, g + 1)
                s.copy(xnT[:, 512 * g:512 * (g + 1)], P8[g][:, :]).then_inc(s_xnT, 1)
            write_maskT(0)
            write_maskT(1)
            write_maskT(2)
            for pair in range(2):
                for b, exponent in enumerate((dnB, dnD)):
                    act.wait_ge(s_dn, 2)
                    s.activation(f_pair[pair][:, :, :, b, HD].rearrange("p h t -> p t h"),
                                 exponent[:, :, 2 * pair:2 * pair + 2], ACT.Exp).then_inc(s_exp, 1)
            write_maskT(3)
            copy_part(0, 0)
            write_maskT(4)
            copy_part(0, 1)
            act.wait_ge(s_dn, 4)
            s.activation(eA[:], tmn[:], ACT.Exp).then_inc(s_exp, 1)
            s.activation(eC[:], tmn2[:], ACT.Exp).then_inc(s_exp, 1)
            write_maskT(5)
            write_maskT(6)
            act.wait_ge(s_const, 1)
            s.activation(warm[:], neg_half[:, 0:1], ACT.Sigmoid).then_inc(s_warm, 1)
            write_maskT(7)

            def step(g):
                unit = STEPS[g]
                blk, h, n = unit // (H * T), unit // T % H, unit % T
                if g >= RS:
                    act.wait_ge(s_z, T + STEPS[g - RS] + 1)
                s.activation(step_t[g % RS], srcb[:, h, blk, :], ACT.Sigmoid, bias=dsteep[:, h, n:n + 1],
                             scale=STEEP).then_inc(s_step, 1)

            def step_of_loop(h, j):
                last_use = ON_ACT[j - RS] + (0 if j >= RS else -T)
                act.wait_ge(s_z, h * T + (T + last_use + 1))
                act.sem_inc(s_turn, 1)
                s.activation(step_t[j % RS], srcb[:, bass.ds(h, 1), 0, :].rearrange("p a n -> p (a n)"),
                             ACT.Sigmoid, bias=dsteep[:, bass.ds(h, 1), ON_ACT[j]], scale=STEEP).then_inc(s_step, 1)

            act.wait_ge(s_srcl[0], 16)
            for j in range(len(ON_ACT)):
                step(j)
                if j in (0, 1):
                    copy_part(1, j)
                if j in (5, 7):
                    copy_part(2, j // 7)
                if j == 9:
                    act.wait_ge(s_src, 4)
                    act.wait_ge(s_srco, 16)
                    act.wait_ge(s_exp, 6)
                    write_maskT(BT)
            for h in range(1, H):
                act.wait_ge(s_srcl[h], 16)
            with act.Fori(1, H) as h:
                for j in range(len(ON_ACT)):
                    step_of_loop(h, j)
                    if j == 1:
                        write_maskT((h + -1, 1))
                    if j == 9:
                        write_maskT((h, 0))
            write_maskT(T - 1)

            def write_x1T(blk, g):
                act.wait_ge(s_tr, 4 + 2 * blk + g + 1)
                if blk > 0:
                    act.wait_ge(s_lg, blk)
                s.copy(x1T[:, 512 * g:512 * (g + 1)], P8[6 + g][:, :]).then_inc(s_xnT, 1)

            def second_rows(blk):
                act.wait_ge(s_xn, T + BT * (blk + 1))
                s.copy(row_k[blk][1][:, :, 0:D], row_k[blk][0][:, :, 0:D]).then_inc(s_rowB, 1)

            def weights(blk):
                act.wait_ge(s_dm, blk + 1)
                for k in range(2):
                    s.activation(row_k[blk][k][:, :, D + 1], gap[:], ACT.Sigmoid, scale=1.0 - 2 * k).then_inc(s_wt, 1)

            for n in range(H * T):
                if H * T + n in STEPS:
                    step(STEPS.index(H * T + n))
                if n in X1T_AT:
                    write_x1T(0, X1T_AT.index(n))
                if n == ROWS2_AT:
                    second_rows(0)
                if n == WEIGHTS_AT:
                    weights(0)
            write_x1T(1, 0)
            write_x1T(1, 1)
            act.wait_ge(s_shift, 1)
            for t in range(BT):
                s.activation(row_k[1][0][:, t, 0:D], x1[:, BT + t, :], ACT.Identity, bias=shift[:, t:t + 1],
                             scale=rstd[:, t:t + 1]).then_inc(s_xn, 1)
            second_rows(1)
            weights(1)
            pad_experts(act, 1)

            def expert_step(tile):
                p = tile + -1
                if p.within(TILES):
                    act.wait_ge(s_hp, p.count(1))
                    wait_from_first(act, s_hid, p.count(-1))
                    s.activation(silu_t[p.c % 2], P8[2 + p.c % 2][:, 0:F], ACT.Silu).then_inc(s_si, 1)
                p = tile + -2
                if p.within(TILES):
                    act.wait_ge(s_t2, p.count(1))
                    wait_from_first(act, s_y, p.count(-1))
                    s.copy(hidT_t[p.c % 2], P8[4 + p.c % 2][:, 0:F]).then_inc(s_hT, 1)
            over_tiles(act, expert_step, 3)

        @block.vector
        def _(dve):
            v = nc.vector
            chain = Chain(dve, s_dve)
            run, post = chain.run, chain.post

            def stats(rows_in, first=0):
                for t in range(rows_in.shape[1]):
                    post(v.bn_stats(stat[:, first + t, :], rows_in[:, t, :]))

            def variance(first=0):
                of = slice(first, first + BT)
                chain.wait()
                post(v.tensor_tensor(mean[:, of], stat[:, of, 1], stat[:, of, 4], ALU.add))
                post(v.tensor_tensor(st1[:, of], stat[:, of, 1], stat[:, of, 4], ALU.subtract))
                post(v.tensor_tensor(st2[:, of], stat[:, of, 2], stat[:, of, 5], ALU.add))
                chain.wait()
                post(v.tensor_scalar(mean[:, of], mean[:, of], 0.5, None, ALU.mult))
                post(v.tensor_tensor(st1[:, of], st1[:, of], st1[:, of], ALU.mult))
                post(v.tensor_scalar(st2[:, of], st2[:, of], 1.0 / D, EPS, ALU.mult, ALU.add))
                chain.wait()
                v.scalar_tensor_tensor(vare[:, of], st1[:, of], 0.25, st2[:, of], ALU.mult, ALU.add).then_inc(s_var, 1)

            def normalised(rows_out, rows_in, t):
                return v.tensor_scalar(rows_out[:, t, :], rows_in[:, t, :], mean[:, t:t + 1], rstd[:, t:t + 1],
                                       ALU.subtract, ALU.mult)

            def mask(tile):
                if isinstance(tile, int):
                    slot, r = adj_slot(tile), tile % 2
                    loads = len([t for t in range(tile + 1) if adj_slot(t) == slot])
                    dve.wait_ge(s_adj[slot], 16 * loads)
                    if tile >= 2:
                        dve.wait_ge(s_mtr, 2 * tile - 2)
                else:
                    h, r = tile
                    slot = adj_slot(BT + r)
                    loads = len([t for t in range(BT + r + 1) if adj_slot(t) == slot])
                    dve.wait_ge(s_adj[slot], h * 16 + 16 * loads)
                    dve.wait_ge(s_mtr, h * 4 + (2 * (BT + r) - 2))
                v.tensor_scalar(mask_t[r], adj_t[slot], 0.0, None, ALU.is_gt).then_inc(s_mask, 1)

            def copy_h(g):
                n = min(3, T - 3 * g)
                dve.wait_ge(s_h, g + 1)
                v.tensor_copy(hh[:, 3 * g:3 * g + n, :],
                              P8[4 + g % 2][:, 0:n * HW].rearrange("p (t c) -> p t c", t=n)).then_inc(s_hs, 1)

            def features(i):
                times_columns(v, *PIECES[i]).then_inc(s_f, 1)

            def second_part(i):
                part, f = parts_of(*PIECES[i])
                dve.wait_ge(s_f, 2 * i + 1)
                dve.wait_ge(s_part, 2 * i + 1)
                v.tensor_tensor(joined(f), joined(f), part[0], ALU.subtract).then_inc(s_f, 1)

            def third_part(i):
                part, f = parts_of(*PIECES[i])
                dve.wait_ge(s_f, 2 * i + 2)
                dve.wait_ge(s_part, 2 * i + 2)
                v.tensor_tensor(part[2], joined(f), part[1], ALU.subtract).then_inc(s_cut, 1)

            dve.sem_inc(s_s0f, 2)
            dve.sem_inc(s_z, T)
            for k in range(2):
                dve.wait_ge(s_xld[k], 16)
                stats(x_sb[:, BT * k:BT * (k + 1), :], BT * k)
                variance(BT * k)
            dve.wait_ge(s_wT, 1)
            v.tensor_copy(wT, P8[4][:, 0:P]).then_inc(s_wTs, 1)
            for half_of_x in range(2):
                dve.wait_ge(s_rstd, half_of_x + 1)
                for t in range(BT * half_of_x, BT * (half_of_x + 1)):
                    normalised(xn, x_sb, t).then_inc(s_xn, 1)
                mask(half_of_x)
            dve.wait_ge(s_wa, 1)
            v.tensor_copy(w_ext[:, D:HW], P8[5][:, 0:2 * H]).then_inc(s_wext, 1)
            mask(2)
            for g in range(6):
                copy_h(g)
            dve.wait_ge(s_hs, 6)
            src, dst = hh[:, :, D:D + H], hh[:, :, D + H:HW]
            v.tensor_reduce(dloc[:], dst.rearrange("p t h -> p h t"), AX.X, ALU.max).then_inc(s_dloc, 1)
            mask(3)
            dve.wait_ge(s_dmax, 1)
            dmax_b = dmax[:, :].unsqueeze(1).to_broadcast([P, T, H])
            post(v.tensor_tensor(dn[:], dst, dmax_b, ALU.subtract))
            post(v.tensor_tensor(tt[:], src, dmax_b, ALU.add))
            chain.wait()
            dve.wait_ge(s_xn, T)
            v.tensor_scalar(dnD[:], dn[:], 0.2, SHIFT, ALU.mult, ALU.add).then_inc(s_dn, 1)
            v.tensor_scalar(dnB[:], dn[:], SHIFT, None, ALU.add).then_inc(s_dn, 1)
            v.tensor_scalar(tmn[:], tt[:], 0.8, 0.0, ALU.mult, ALU.min).then_inc(s_dn, 1)
            v.tensor_scalar(tmn2[:], tt[:], -0.8, 0.0, ALU.mult, ALU.min).then_inc(s_dn, 1)
            post(v.tensor_scalar(ndst[:].rearrange("p h t -> p t h"), dst, -1.0, None, ALU.mult))
            post(v.tensor_scalar(dsteep[:].rearrange("p h t -> p t h"), dst, STEEP, None, ALU.mult))
            mask(4)
            dve.wait_ge(s_exp, 2)
            features(0)
            for c in range(4):
                dve.wait_ge(s_src, c + 1)
                v.tensor_copy(src_rows[:, 512 * c:512 * (c + 1)], P8[c][0:H, :]).then_inc(s_srcs, 1)
            mask(5)
            second_part(0)
            mask(6)
            mask(7)
            third_part(0)
            features(1)

            def z1(blk, h, n):
                known = isinstance(h, int)
                u = h * T + (blk * H * T + n)
                dve.wait_ge(s_zu, u + 1)
                z0 = maskT[:, blk, n, :]
                if n in (ON_DVE if blk == 0 else ON_DVE_2[h]):
                    src_row = srcb[:, h, blk, :] if known else \
                        srcb[:, bass.ds(h, 1), blk, :].rearrange("p a n -> p (a n)")
                    nd = ndst[:, h, n:n + 1] if known else ndst[:, bass.ds(h, 1), n]
                    v.scalar_tensor_tensor(z_t[n % RZ], src_row, nd, z0, ALU.is_gt, ALU.mult).then_inc(s_z, 1)
                else:
                    g = STEPS.index(u) if known else h * len(ON_ACT) + ON_ACT.index(n)
                    dve.wait_ge(s_step, g + 1)
                    place = g if known else ON_ACT.index(n)
                    v.tensor_tensor(z_t[n % RZ], step_t[place % RS], z0, ALU.mult).then_inc(s_z, 1)

            def s1_sum(blk, h):
                for b in range(4):
                    dve.wait_ge(s_zu, (h + blk * H) * T + (RZ + T))
                    to = s1[blk][:, h, 2 * b:2 * b + 2, :] if isinstance(h, int) else \
                        s1[blk][:, bass.ds(h, 1), 2 * b:2 * b + 2, :].rearrange("p a i c -> p (a i) c")
                    v.tensor_reduce(to, P8[b][:, 0:6 * C2].rearrange("p (i k c) -> p i c k", i=2, k=3),
                                    AX.X, ALU.add).then_inc(s_acc, 1)

            def s0_sum(tile, r):
                dve.wait_ge(s_s0, tile + 1)
                v.tensor_reduce(sums_at(tile), P8[4 + r][:, 0:3 * H * C1].rearrange("p (h k c) -> p h c k", h=H, k=3),
                                AX.X, ALU.add).then_inc(s_s0f, 1)

            dve.wait_ge(s_srcl[0], 16)
            dve.wait_ge(s_mask, BT)
            dve.wait_ge(s_mT, 2 * BT)
            chain.wait()
            dve.wait_ge(s_exp, 4)
            for n in range(T):
                z1(0, 0, n)
                if n in (0, 7):
                    second_part(1 + n // 7)
                if n in (1, 10):
                    third_part(1 + n // 10)
                if n == 4:
                    features(2)
                if n == 13:
                    dve.wait_ge(s_cut2, 4)
                    s0_sum(0, 0)
                if n == T - 1:
                    s0_sum(1, 1)
                if n == 5:
                    dve.wait_ge(s_xn, T)
                    mask(BT)
                if n == 9:
                    mask(BT + 1)
            for h in range(1, H):
                dve.wait_ge(s_srcl[h], 16)
            with dve.Fori(1, H) as h:
                for n in range(T):
                    z1(0, h, n)
                    if n == 1:
                        s1_sum(0, h + -1)
                    if n == 1:
                        mask((h, 0))
                    if n == 7:
                        s0_sum(h * 2, 0)
                    if n == 8:
                        mask((h, 1))
                    if n == 15:
                        s0_sum(h * 2 + 1, 1)

            def per_head(column):
                return column.to_broadcast([P, BT, H, HD])

            def ratios(blk, heads):
                of, width = slice(BT * blk, BT * (blk + 1)), heads.stop - heads.start
                run(v.reciprocal(rden[:, of, heads], S0[:, of, heads, HD]))
                run(v.tensor_tensor(gat.rearrange("p t (h c) -> p t h c", h=H)[:, :, heads, :], S0[:, of, heads, 0:HD],
                                    rden[:, of, heads].unsqueeze(3).to_broadcast([P, BT, width, HD]), ALU.mult))

            def x1_of(blk):
                return x1[:, BT * blk:BT * (blk + 1), :]

            def scaled_attention():
                for t in range(BT):
                    post(v.scalar_tensor_tensor(normed[:, t, :], gat[:, t, :], mean[:, t:t + 1], gam[:, :],
                                                ALU.subtract, ALU.mult))

            def residual(blk):
                dve.wait_ge(s_rstd, 3 + 2 * blk)
                chain.wait()
                for t in range(BT):
                    v.scalar_tensor_tensor(x1_of(blk)[:, t, :], normed[:, t, :], rstd[:, t:t + 1],
                                           x_again[:, BT * blk + t, :], ALU.mult, ALU.add).then_inc(s_x1, 1)

            def destinations(blk):
                of = slice(BT * blk, BT * (blk + 1))
                v.tensor_copy(row_k[blk][0][:, :, D].bitcast(I32), goes_to[:, 0, of]).then_inc(s_rowA, 1)
                v.tensor_copy(row_k[blk][1][:, :, D].bitcast(I32), goes_to[:, 1, of]).then_inc(s_rowC, 1)

            def centred_logits(blk):
                columns = gcs[:, :].unsqueeze(1).to_broadcast([P, BT, E])
                run(v.tensor_tensor(eq, over_e(mean[:, 0:BT]), columns, ALU.mult))
                dve.wait_ge(s_lg, blk + 1)
                run(v.tensor_tensor(eq, P8[6][:, 0:BT * E].rearrange("p (t e) -> p t e", t=BT), eq, ALU.subtract))

            def logits(blk):
                dve.wait_ge(s_rstd, 4 + 2 * blk)
                run(v.tensor_tensor(lg, eq, over_e(rstd[:, 0:BT]), ALU.mult))
                run(v.tensor_tensor(lg, lg, gb[:, :].unsqueeze(1).to_broadcast([P, BT, E]), ALU.add))

            def over_e(one_per_token):
                return one_per_token.unsqueeze(2).to_broadcast([P, BT, E])
            order = first_e[:, :].unsqueeze(1).to_broadcast([P, BT, E])

            def choose(logits, top, chosen):
                run(v.tensor_reduce(top[:], logits, AX.X, ALU.max))
                run(v.tensor_tensor(eq, logits, over_e(top[:, :]), ALU.is_equal))
                run(v.tensor_tensor(eq, eq, order, ALU.mult))
                run(v.tensor_reduce(key1[:], eq, AX.X, ALU.max))
                run(v.tensor_tensor(chosen, order, over_e(key1[:, :]), ALU.is_equal))

            def second_logits():
                run(v.scalar_tensor_tensor(lg2, M1, -BIG, lg, ALU.mult, ALU.add))

            def chosen(blk):
                v.tensor_tensor(Mb[:, BT * blk:BT * (blk + 1), :], M1, M2, ALU.add).then_inc(s_M, 1)
                if blk > 0:
                    dve.wait_ge(s_wt, 2 * blk)
                v.tensor_tensor(gap[:], m1[:], m2[:], ALU.subtract).then_inc(s_dm, 1)

            def slots(blk):
                dve.wait_ge(s_rank, blk + 1)
                run(v.tensor_tensor(eq, P8[7][:, 0:BT * E].rearrange("p (t e) -> p t e", t=BT),
                                    region[:, :].unsqueeze(1).to_broadcast([P, BT, E]), ALU.add))
                for k, M in enumerate((M1, M2)):
                    run(v.tensor_tensor(M, M, eq, ALU.mult))
                    run(v.tensor_reduce(slot_f[:, k, :], M, AX.X, ALU.add))
                    v.tensor_copy(slot_i[:, blk, k, :], slot_f[:, k, :]).then_inc(s_slot, 1)

            dve.wait_ge(s_mT, 2 * T)
            for n in range(H * T):
                h, jt = divmod(n, T)
                z1(1, h, jt)
                if jt == 0:
                    s1_sum(0 if h == 0 else 1, (h - 1) % H)
                if n in S0_AT:
                    tile = BT + S0_AT.index(n)
                    s0_sum(tile, tile % 2)
                if n == DIV_AT:
                    dve.wait_ge(s_num, 1)
                    dve.wait_ge(s_s0, BT)
                    ratios(0, slice(0, H))
                if n == DIV_AT + 1:
                    stats(gat)
                if n == DIV_AT + 2:
                    variance()
                if n == STATS_AT:
                    dve.wait_ge(s_x1, BT)
                    stats(x1_of(0))
                if n == STATS_AT + 1:
                    variance()
                if n == CHOOSE_AT - 1:
                    destinations(0)
                if n == CHOOSE_AT:
                    dve.wait_ge(s_gcs, 1)
                    centred_logits(0)
                    logits(0)
                if n == CHOOSE_AT + 1:
                    choose(lg, m1, M1)
                if n == CHOOSE_AT + 2:
                    second_logits()
                if n == CHOOSE_AT + 3:
                    choose(lg2, m2, M2)
                    chosen(0)
                if n == SLOTS_AT:
                    slots(0)
                if n == DIV2_AT:
                    dve.wait_ge(s_num, 2)
                    ratios(1, slice(0, H - 1))
            s1_sum(1, H - 1)
            dve.wait_ge(s_acc, BLK * 4 * H)
            dve.wait_ge(s_s0f, 2 + T)

            numerators(v, chain, 1, slice(H - 1, H))
            dve.wait_ge(s_num, 3)
            ratios(1, slice(H - 1, H))
            stats(gat)
            dve.wait_ge(s_xn, T + BT)
            variance()
            scaled_attention()
            dve.wait_ge(s_xb, 1)
            residual(1)
            dve.wait_ge(s_x1, 2 * BT)
            stats(x1_of(1))
            variance()
            destinations(1)
            centred_logits(1)
            dve.wait_ge(s_rstd, 6)
            v.scalar_tensor_tensor(shift[:], mean[:, 0:BT], -1.0, rstd[:, 0:BT], ALU.mult, ALU.mult
                                   ).then_inc(s_shift, 1)
            logits(1)
            choose(lg, m1, M1)
            second_logits()
            choose(lg2, m2, M2)
            chosen(1)
            slots(1)
            dve.wait_ge(s_rank, 3)
            run(v.tensor_copy(cnt[:], P8[5][:, 0:E]))
            run(v.tensor_tensor(pad_f[:], cnt[0:1, :], region[0:1, :], ALU.add))
            v.tensor_copy(pad_at[:], pad_f[:]).then_inc(s_pads, 1)
            run(v.tensor_tensor(big3, cnt[:, :].unsqueeze(2).to_broadcast([P, E, T]),
                                k128[:, :].unsqueeze(1).to_broadcast([P, E, T]), ALU.is_gt))
            run(v.tensor_reduce(ntile[:], big3, AX.X, ALU.add))
            run(v.tensor_tensor(tri, lt_e[:], ntile[:, :].unsqueeze(1).to_broadcast([P, E, E]), ALU.mult))
            run(v.tensor_reduce(base[:], tri, AX.X, ALU.add))
            post(v.tensor_tensor(endq[:], base[:], ntile[:], ALU.add))
            post(v.scalar_tensor_tensor(off_e[:], base[0:1, :], -float(P), region[0:1, :], ALU.mult, ALU.add))
            chain.wait()
            run(v.tensor_tensor(cmpq, endq[0:1, :].unsqueeze(1).to_broadcast([1, Q, E]),
                                qtile[0:1, :].unsqueeze(2).to_broadcast([1, Q, E]), ALU.is_le))
            run(v.tensor_reduce(eid_f[:], cmpq, AX.X, ALU.add))
            run(v.tensor_tensor(hotq, e_row[0:1, :].unsqueeze(1).to_broadcast([1, Q, E]),
                                eid_f[0:1, :].unsqueeze(2).to_broadcast([1, Q, E]), ALU.is_equal))
            run(v.tensor_tensor(hotq, hotq, off_e[0:1, :].unsqueeze(1).to_broadcast([1, Q, E]), ALU.mult))
            post(v.tensor_reduce(at_f[:], hotq, AX.X, ALU.add))
            run(v.tensor_scalar(live[:], eid_f[:], float(E), None, ALU.is_lt))
            post(v.scalar_tensor_tensor(at_f[:], qtile[:], float(P), at_f[:], ALU.mult, ALU.add))
            post(v.tensor_scalar(eid_f[:], eid_f[:], float(E - 1), None, ALU.min))
            chain.wait()
            run(v.tensor_scalar(at_f[:], at_f[:], pad_f[0:1, 0:1], None, ALU.subtract))
            run(v.tensor_tensor(at_f[:], at_f[:], live[:], ALU.mult))
            run(v.tensor_scalar(at_f[:], at_f[:], pad_f[0:1, 0:1], None, ALU.add))
            run(v.tensor_copy(place[:], at_f[:]))
            v.tensor_copy(eid[:, 4:4 + Q], eid_f[:]).then_inc(s_eid, 1)

            def expert_step(tile):
                if tile.within(TILES):
                    dve.wait_ge(s_t1, tile.count(1))
                    wait_from_first(dve, s_hp, tile.count(-3))
                    v.tensor_copy(xgT_t[tile.c % 4], P8[tile.c % 2][:, 0:P]).then_inc(s_xgT, 1)
                p = tile + -1
                if p.within(TILES):
                    dve.wait_ge(s_si, p.count(1))
                    wait_from_first(dve, s_t2, p.count(-1))
                    v.tensor_tensor(hid_t[p.c % 2], silu_t[p.c % 2], P8[2 + p.c % 2][:, F:2 * F],
                                    ALU.mult).then_inc(s_hid, 1)
                p = tile + -3
                if p.within(TILES):
                    dve.wait_ge(s_y, p.count(1))
                    wait_from_first(dve, s_yst[p.c % 4], p.round(4) * 16)
                    v.tensor_scalar(y_t[p.c % 4], P8[6 + p.c % 2][:, 0:D], xg_t[p.c % RING][:, D + 1:D + 2], None,
                                    ALU.mult).then_inc(s_ys, 1)
            over_tiles(dve, expert_step, 3)

            n = T // G
            for g in range(G):
                part = slice(n * g, n * (g + 1))
                dve.wait_ge(s_gath[g], 16)
                run(v.tensor_tensor(tmp[:, part, :], y_pair[:, part, 0:D], y_pair[:, part, D:2 * D], ALU.add))
                v.tensor_tensor(tmp[:, part, :], tmp[:, part, :], x1[:, part, :], ALU.add).then_inc(s_fin, 1)

        @block.tensor
        def _(pe):
            mm, tp = nc.tensor.matmul, nc.tensor.transpose
            pe.wait_ge(s_wld, 16)
            pe.wait_ge(s_const, 1)
            tp(P8[4][:, 0:P], w_ext[:, 0:D], ident[:]).then_inc(s_wT, 1)

            def transpose_mask(tile):
                for b in range(2):
                    if isinstance(tile, int):
                        r = tile % 2
                        pe.wait_ge(s_mask, tile + 1)
                        if tile > 0:
                            pe.wait_ge(s_mT, 2 * tile - 1 + b)
                    else:
                        h, r = tile
                        pe.wait_ge(s_mask, h * 2 + (BT + r + 1))
                        pe.wait_ge(s_mT, h * 4 + (2 * (BT + r) - 1 + b))
                    for j in range(8):
                        last = tp(P8[6 + b][:, 64 * j:64 * (j + 1)].bitcast(BF16),
                                  mask_t[r][:, P * (8 * b + j):P * (8 * b + j + 1)], ident_b[:])
                    last.then_inc(s_mtr, 1)

            def h_products(g):
                if g >= 2:
                    pe.wait_ge(s_hs, g - 1)
                for t in range(3 * g, min(3 * g + 3, T)):
                    last = mm(P8[4 + g % 2][:, HW * (t - 3 * g):HW * (t - 3 * g + 1)], xnT[:, P * t:P * (t + 1)],
                              w_ext[:, :], start=True, stop=True)
                last.then_inc(s_h, 1)

            def src_product(c):
                mm(P8[c][0:H, :], w_ext[:, D:D + H], xnT[:, 512 * c:512 * (c + 1)], start=True, stop=True
                   ).then_inc(s_src, 1)

            def s0_products(tile, r, j_tiles):
                if j_tiles[0] == 0:
                    pe.wait_ge(s_s0f, tile + 1)
                blk = tile // BT if isinstance(tile, int) else 0
                rows = slice(P * (tile % BT), P * (tile % BT + 1)) if isinstance(tile, int) else bass.ds(tile * P, P)
                for j in j_tiles:
                    last = mm(P8[4 + r][:, 0:3 * H * C1], maskT[:, blk, j, rows],
                              feat[:, :, j, :, C1:C2], start=(j == 0), stop=(j == T - 1))
                if j_tiles[-1] == T - 1:
                    last.then_inc(s_s0, 1)

            def pair(k):
                return range(2 * k, 2 * k + 2)

            def z1_products(blk, h, n):
                u = h * T + (blk * H * T + n)
                pe.wait_ge(s_z, u + (T + 1))
                known = isinstance(h, int)
                moving = feat[:, h, n, :, :].rearrange("p k c -> p (k c)") if known else \
                    feat[:, bass.ds(h, 1), n, :, :].rearrange("p a k c -> p (a k c)")
                for i in range(BT):
                    b = i // 2
                    if n == 0 and i % 2 == 0 and not (known and blk == h == 0):
                        pe.wait_ge(s_acc, (h + blk * H) * 4 + (b - 3))
                    last = mm(P8[b][:, 3 * C2 * (i % 2):3 * C2 * (i % 2 + 1)], z_t[n % RZ][:, P * i:P * (i + 1)],
                              moving, start=(n == 0 and i % 2 == 0), stop=(n == T - 1), skip_group_check=True)
                last.then_inc(s_zu, 1)

            pe.sem_inc(s_zu, RZ)
            for g in range(4):
                pe.wait_ge(s_xn, 4 * (g + 1))
                for t in range(4):
                    last = tp(P8[g][:, P * t:P * (t + 1)], xn[:, 4 * g + t, :], ident[:])
                last.then_inc(s_tr, 1)
            pe.wait_ge(s_wTs, 1)
            pe.wait_ge(s_ald, 16 * 2 * H)
            mm(P8[5][:, 0:2 * H], wT, a_blk[:], start=True, stop=True).then_inc(s_wa, 1)
            transpose_mask(0)
            pe.wait_ge(s_xnT, 4)
            pe.wait_ge(s_wext, 1)
            for g in range(2):
                h_products(g)
            transpose_mask(1)
            for g in range(2, 6):
                h_products(g)
            transpose_mask(2)
            for c in range(2):
                src_product(c)
            transpose_mask(3)
            for c in range(2, 4):
                src_product(c)
            for tile in range(4, BT):
                transpose_mask(tile)

            pe.wait_ge(s_srcs, 4)
            pe.wait_ge(s_hs, 6)
            pe.wait_ge(s_cut, 1)
            for n in range(T):
                z1_products(0, 0, n)
                if n == 3:
                    pe.wait_ge(s_cut, 2)
                    pe.wait_ge(s_cut2, 2)
                for m in range(3 * (n - 3), min(3 * (n - 2), 2 * T)):
                    if m >= 0:
                        s0_products(m // T, m // T, range(m % T, m % T + 1))
                if n == 4:
                    transpose_mask(BT)
                if n == 9:
                    transpose_mask(BT + 1)
            pe.wait_ge(s_cut, 3)
            pe.wait_ge(s_cut2, 4)
            with pe.Fori(1, H) as h:
                s0_products(h * 2, 0, range(T))
                for n in range(T):
                    z1_products(0, h, n)
                    if n < 8:
                        s0_products(h * 2 + 1, 1, pair(n))
                    if n == 1:
                        transpose_mask((h, 0))
                    if n == 9:
                        transpose_mask((h, 1))

            def transpose_rows(blk, g):
                pe.wait_ge(s_x1, BT * blk + 4 * (g + 1))
                for t in range(4):
                    last = tp(P8[6 + g][:, P * t:P * (t + 1)], x1[:, BT * blk + 4 * g + t, :], ident[:])
                last.then_inc(s_tr, 1)

            def logits(blk):
                for t in range(BT):
                    if t % 4 == 0:
                        pe.wait_ge(s_xnT, 4 + 2 * blk + t // 4 + 1)
                    last = mm(P8[6][:, E * t:E * (t + 1)], x1T[:, P * t:P * (t + 1)], gw[:], start=True, stop=True)
                last.then_inc(s_lg, 1)

            def ranks(blk):
                first = BT * blk
                if blk > 0:
                    pe.wait_ge(s_slot, 2)
                for t in range(first):
                    mm(P8[7][:, 0:BT * E].rearrange("p (t e) -> p t e", e=E), ones_b[:],
                       Mb[:, t:t + 1, :].to_broadcast([P, BT, E]), start=(t == 0), stop=False)
                pe.wait_ge(s_M, blk + 1)
                mm(P8[7][:, 0:BT * E], before[:], Mb[:, first:first + BT, :].rearrange("p t e -> p (t e)"),
                   start=(blk == 0), stop=False)
                for n in range(1, BT):
                    t = first + n - 1
                    last = mm(P8[7][:, E * n:BT * E].rearrange("p (t e) -> p t e", e=E), ones_b[:],
                              Mb[:, t:t + 1, :].to_broadcast([P, BT - n, E]), start=False, stop=(n == BT - 1))
                last.then_inc(s_rank, 1)

            pe.wait_ge(s_mT, 2 * T)
            pe.wait_ge(s_gld, 64)
            for n in range(H * T):
                if n in S0_BEFORE:
                    s0_products(S0_BEFORE[n], S0_BEFORE[n] % 2, range(T))
                z1_products(1, n // T, n % T)
                for first, tile in S0_FROM.items():
                    if 0 <= n - first < T // 2:
                        s0_products(tile, tile % 2, pair(n - first))
                if n == TR_AT:
                    transpose_rows(0, 0)
                    transpose_rows(0, 1)
                if n == LOGITS_AT:
                    logits(0)
                if n == RANKS_AT:
                    ranks(0)
            transpose_rows(1, 0)
            transpose_rows(1, 1)
            logits(1)
            ranks(1)
            for t in range(T):
                last = mm(P8[5][:, 0:E], ones_b[:], Mb[:, t, :], start=(t == 0), stop=(t == T - 1))
            last.then_inc(s_rank, 1)

            pe.wait_ge(s_w12, 32)
            pe.wait_ge(s_w3, 16)
            pe.wait_ge(s_eid, 1)

            experts = [pe.alloc_register(f"expert{n}") for n in range(8)]

            def load_experts(tile):
                at = slice(tile.count(), tile.count(8)) if tile.known() else bass.ds(tile.count(), 8)
                pe.load(experts, eid[0:1, at])

            def expert_of(n):
                return pe.snap(experts[n], min_val=0, max_val=E - 1)

            load_experts(Tile(0, 0))

            def expert_step(tile):
                if tile.within(TILES):
                    r = tile.c % RING
                    pe.wait_ge(s_xg[r], tile.round(RING, 1) * 16)
                    wait_from_first(pe, s_xgT, tile.count(-1))
                    tp(P8[tile.c % 2][:, 0:P], xg_t[r][:, 0:D], ident[:]).then_inc(s_t1, 1)
                p = tile + -1
                if p.within(TILES):
                    e = expert_of(3 + tile.c % 4)
                    pe.wait_ge(s_xgT, p.count(1))
                    wait_from_first(pe, s_hid, p.count(-1))
                    mm(P8[2 + p.c % 2][:, :], xgT_t[p.c % 4], R1[:, bass.ds(e * (2 * F), 2 * F)],
                       start=True, stop=True).then_inc(s_hp, 1)
                if (tile + -3).within(TILES):
                    e = expert_of(1 + tile.c % 4)
                if tile.c % 4 == 3:
                    load_experts(tile + 1)
                p = tile + -2
                if p.within(TILES):
                    pe.wait_ge(s_hid, p.count(1))
                    wait_from_first(pe, s_hT, p.count(-1))
                    for c in range(FC):
                        last = tp(P8[4 + p.c % 2][:, P * c:P * (c + 1)], hid_t[p.c % 2][:, P * c:P * (c + 1)], ident[:])
                    last.then_inc(s_t2, 1)
                p = tile + -3
                if p.within(TILES):
                    pe.wait_ge(s_hT, p.count(1))
                    wait_from_first(pe, s_ys, p.count(-1))
                    for c in range(FC):
                        last = mm(P8[6 + p.c % 2][:, 0:D], hidT_t[p.c % 2][:, P * c:P * (c + 1)],
                                  w3_all[:, bass.ds(e * (FC * D) + c * D, D)], start=(c == 0), stop=(c == FC - 1))
                    last.then_inc(s_y, 1)
            over_tiles(pe, expert_step, 3)


_INS = ["x", "adj", "L0_gnn_W", "L0_gnn_a", "L0_gnn_gamma", "L0_gnn_beta", "L0_ffn_gate_w", "L0_ffn_gate_b",
        "L0_ffn_w1", "L0_ffn_w2", "L0_ffn_w3"]


def kernel(**inputs):
    import numpy as np
    import concourse.bacc as bacc
    from concourse.bass_utils import run_bass_kernel_spmd

    nc = bacc.Bacc("TRN2", target_bir_lowering=False, num_devices=1)
    arrays, args = {}, []
    for name in _INS:
        array = np.ascontiguousarray(inputs[name])
        arrays[name] = array
        args.append(nc.dram_tensor(name, array.shape, F32, kind="ExternalInput").ap())
    out = nc.dram_tensor("out", inputs["x"].shape, F32, kind="ExternalOutput").ap()
    build(nc, *args, out)
    got = run_bass_kernel_spmd(nc, [arrays], core_ids=[0])
    return got.results[0]["out"]
```
